# Optimizing a Trainium2 kernel written in Bass

```python
import numpy as np
import jax
import jax.numpy as jnp

def _softmax(x, axis=-1):
    return jax.nn.softmax(x, axis=axis)

def _gelu(x):
    return jax.nn.gelu(x, approximate=True)

def _silu(x):
    return jax.nn.silu(x)

def _sigmoid(x):
    return jax.nn.sigmoid(x)

def _layernorm(x, axis=-1, eps=1e-05):
    m = jnp.mean(x, axis=axis, keepdims=True)
    v = jnp.var(x, axis=axis, keepdims=True)
    return (x - m) / jnp.sqrt(v + eps)

def _scatter_add(tgt, idx, src, axis=0):
    return tgt.at[idx].add(src)

def _segment_sum(src, seg, n):
    return jax.ops.segment_sum(src, seg, n)
kernel_name = 'mk_perceiver_d1_seqx_r2_e246e9'

def setup_inputs(seed: int=0):
    np.random.seed(seed)
    _w = jnp.asarray

    def _rec_inputs():
        import jax
        import jax.numpy as jnp
        _rk = jax.random.key(seed)
        x = 7.22e-05 + 1 * jax.random.normal(jax.random.fold_in(_rk, 1), (8, 64, 512), jnp.float32)
        _lenS = 64 - jax.random.randint(jax.random.fold_in(_rk, 7), (8,), 0, max(1, 64 // 4) + 1, jnp.int32)
        _lenS2 = 1601 - jax.random.randint(jax.random.fold_in(_rk, 8), (8,), 0, max(1, 1601 // 4) + 1, jnp.int32)
        _ctx_1024P = jax.random.normal(jax.random.fold_in(_rk, 11), (8, 16, 512), jnp.float32)
        _ctx_1024c = jax.random.dirichlet(jax.random.fold_in(_rk, 511), 0.3 * jnp.ones((16,), jnp.float32), (8, 1601))
        _ctx_1024t = jnp.einsum('bsk,bkd->bsd', _ctx_1024c, _ctx_1024P)
        _ctx_1024t = _ctx_1024t * jax.lax.rsqrt(jnp.mean(jnp.square(_ctx_1024t)) + 1e-12) * 0.953939
        ctx_1024 = 4.13588e-05 + 0.999923 * (_ctx_1024t + 0.3 * jax.random.normal(jax.random.fold_in(_rk, 611), (8, 1601, 512), jnp.float32))
        return (x, ctx_1024)
    x, ctx_1024 = _rec_inputs()

    def _L0_xattn_setup():
        import jax, jax.numpy as jnp
        import numpy as np
        B, SQ, SKV, E, H = (4, 1024, 1024, 512, 16)
        HD = E // H

        def stablemax(x):
            s = jnp.where(x >= 0, x + 1.0, 1.0 / (1.0 - x))
            return s / jnp.sum(s, axis=-1, keepdims=True)
        key = jax.random.key(seed)
        ks = jax.random.split(key, 6)
        scale = 1.0 / np.sqrt(E)
        return {'query': jax.random.normal(ks[0], (B, SQ, E), jnp.float32), 'key_value': jax.random.normal(ks[1], (B, SKV, E), jnp.float32), 'Wq': jax.random.normal(ks[2], (E, E), jnp.float32) * scale, 'bq': jnp.zeros((E,), jnp.float32), 'Wk': jax.random.normal(ks[3], (E, E), jnp.float32) * scale, 'bk': jnp.zeros((E,), jnp.float32), 'Wv': jax.random.normal(ks[4], (E, E), jnp.float32) * scale, 'bv': jnp.zeros((E,), jnp.float32), 'Wo': jax.random.normal(ks[5], (E, E), jnp.float32) * scale, 'bo': jnp.zeros((E,), jnp.float32)}
    _L0_xattn_all = _L0_xattn_setup()
    _L0_xattn_in = {k: v for k, v in _L0_xattn_all.items() if k in ('Wq', 'bq', 'Wk', 'bk', 'Wv', 'bv', 'Wo', 'bo')}
    del _L0_xattn_all

    def _L0_attn_setup():
        import jax, jax.numpy as jnp
        import numpy as np
        B, T, C = (4, 1024, 512)
        NQ, D = (8, C // 8)
        key = jax.random.key(seed)
        ks = jax.random.split(key, 6)
        s = 0.02
        return {'x': jax.random.normal(ks[0], (B, T, C), dtype=jnp.float32), 'Wk': jax.random.normal(ks[1], (C, D), dtype=jnp.float32) * s, 'Wv': jax.random.normal(ks[2], (C, D), dtype=jnp.float32) * s, 'Wq': jax.random.normal(ks[3], (NQ, C, D), dtype=jnp.float32) * s, 'Wp': jax.random.normal(ks[4], (NQ * D, C), dtype=jnp.float32) * s, 'bp': jnp.zeros((C,), dtype=jnp.float32)}
    _L0_attn_all = _L0_attn_setup()
    _L0_attn_in = {k: v for k, v in _L0_attn_all.items() if k in ('Wk', 'Wv', 'Wq', 'Wp', 'bp')}
    del _L0_attn_all

    def _L0_ffn_setup():
        import jax, jax.numpy as jnp
        import numpy as np
        D_MODEL = 512
        HIDDEN = 2048
        NUM_EXPERTS = 8
        TOP_K = 2
        NUM_SHARED = 2

        def _gelu(x):
            return jax.nn.gelu(x, approximate=False)
        key = jax.random.key(seed)
        ks = jax.random.split(key, 12)
        s = 0.02
        return {'x': jax.random.normal(ks[0], (2, 1024, D_MODEL), dtype=jnp.float32), 'rW': jax.random.normal(ks[1], (D_MODEL, NUM_EXPERTS), dtype=jnp.float32) * s, 'rb': jnp.zeros((NUM_EXPERTS,), dtype=jnp.float32), 'W1': jax.random.normal(ks[2], (NUM_EXPERTS, D_MODEL, HIDDEN), dtype=jnp.float32) * s, 'b1': jnp.zeros((NUM_EXPERTS, HIDDEN), dtype=jnp.float32), 'W2': jax.random.normal(ks[3], (NUM_EXPERTS, HIDDEN, D_MODEL), dtype=jnp.float32) * s, 'b2': jnp.zeros((NUM_EXPERTS, D_MODEL), dtype=jnp.float32), 'sW1': jax.random.normal(ks[4], (NUM_SHARED, D_MODEL, HIDDEN), dtype=jnp.float32) * s, 'sb1': jnp.zeros((NUM_SHARED, HIDDEN), dtype=jnp.float32), 'sW2': jax.random.normal(ks[5], (NUM_SHARED, HIDDEN, D_MODEL), dtype=jnp.float32) * s, 'sb2': jnp.zeros((NUM_SHARED, D_MODEL), dtype=jnp.float32)}
    _L0_ffn_all = _L0_ffn_setup()
    _L0_ffn_in = {k: v for k, v in _L0_ffn_all.items() if k in ('rW', 'rb', 'W1', 'b1', 'W2', 'b2', 'sW1', 'sb1', 'sW2', 'sb2')}
    del _L0_ffn_all
    return {'x': x, 'ctx_1024': ctx_1024, 'L0_xattn_Wq': _L0_xattn_in['Wq'], 'L0_xattn_bq': _L0_xattn_in['bq'], 'L0_xattn_Wk': _L0_xattn_in['Wk'], 'L0_xattn_bk': _L0_xattn_in['bk'], 'L0_xattn_Wv': _L0_xattn_in['Wv'], 'L0_xattn_bv': _L0_xattn_in['bv'], 'L0_xattn_Wo': _L0_xattn_in['Wo'], 'L0_xattn_bo': _L0_xattn_in['bo'], 'L0_attn_Wk': _L0_attn_in['Wk'], 'L0_attn_Wv': _L0_attn_in['Wv'], 'L0_attn_Wq': _L0_attn_in['Wq'], 'L0_attn_Wp': _L0_attn_in['Wp'], 'L0_attn_bp': _L0_attn_in['bp'], 'L0_ffn_rW': _L0_ffn_in['rW'], 'L0_ffn_rb': _L0_ffn_in['rb'], 'L0_ffn_W1': _L0_ffn_in['W1'], 'L0_ffn_b1': _L0_ffn_in['b1'], 'L0_ffn_W2': _L0_ffn_in['W2'], 'L0_ffn_b2': _L0_ffn_in['b2'], 'L0_ffn_sW1': _L0_ffn_in['sW1'], 'L0_ffn_sb1': _L0_ffn_in['sb1'], 'L0_ffn_sW2': _L0_ffn_in['sW2'], 'L0_ffn_sb2': _L0_ffn_in['sb2']}

def reference(x, ctx_1024, L0_xattn_Wq, L0_xattn_bq, L0_xattn_Wk, L0_xattn_bk, L0_xattn_Wv, L0_xattn_bv, L0_xattn_Wo, L0_xattn_bo, L0_attn_Wk, L0_attn_Wv, L0_attn_Wq, L0_attn_Wp, L0_attn_bp, L0_ffn_rW, L0_ffn_rb, L0_ffn_W1, L0_ffn_b1, L0_ffn_W2, L0_ffn_b2, L0_ffn_sW1, L0_ffn_sb1, L0_ffn_sW2, L0_ffn_sb2):
    import jax
    import jax.numpy as jnp

    def _L0_xattn_ref(query, key_value, Wq, bq, Wk, bk, Wv, bv, Wo, bo):
        import jax, jax.numpy as jnp
        import numpy as np
        B, SQ, SKV, E, H = (4, 1024, 1024, 512, 16)
        HD = E // H

        def stablemax(x):
            s = jnp.where(x >= 0, x + 1.0, 1.0 / (1.0 - x))
            return s / jnp.sum(s, axis=-1, keepdims=True)
        b = query.shape[0]
        q = query @ Wq.T + bq
        k = key_value @ Wk.T + bk
        v = key_value @ Wv.T + bv
        q = q.reshape(b, -1, H, HD).transpose(0, 2, 1, 3)
        k = k.reshape(b, -1, H, HD).transpose(0, 2, 1, 3)
        v = v.reshape(b, -1, H, HD).transpose(0, 2, 1, 3)
        scores = jnp.einsum('bhqd,bhkd->bhqk', q, k) / np.sqrt(HD).astype(np.float32)
        attn = stablemax(scores)
        context = jnp.einsum('bhqk,bhkd->bhqd', attn, v)
        context = context.transpose(0, 2, 1, 3).reshape(b, -1, E)
        return context @ Wo.T + bo

    def _L0_attn_ref(x, Wk, Wv, Wq, Wp, bp):
        import jax, jax.numpy as jnp
        import numpy as np
        B, T, C = (4, 1024, 512)
        NQ, D = (8, C // 8)
        b, t, c = x.shape
        scale = c ** (-0.5)
        k = x @ Wk
        v = x @ Wv
        q = jnp.einsum('btc,qcd->bqtd', x, Wq)
        wei = jnp.einsum('bqtd,bsd->bqts', q, k) * scale
        causal = jnp.tril(jnp.ones((t, t), dtype=bool))
        wei = jnp.where(causal, wei, -jnp.inf)
        wei = jax.nn.softmax(wei, axis=-1)
        out = jnp.einsum('bqts,bsd->btqd', wei, v)
        out = out.reshape(b, t, -1)
        return out @ Wp + bp

    def _L0_ffn_ref(x, rW, rb, W1, b1, W2, b2, sW1, sb1, sW2, sb2):
        import jax, jax.numpy as jnp
        import numpy as np
        D_MODEL = 512
        HIDDEN = 2048
        NUM_EXPERTS = 8
        TOP_K = 2
        NUM_SHARED = 2

        def _gelu(x):
            return jax.nn.gelu(x, approximate=False)
        B, L, D = x.shape
        xf = x.reshape(-1, D)
        sh = _gelu(jnp.einsum('td,sdh->sth', xf, sW1) + sb1[:, None, :])
        shared = jnp.einsum('sth,shd->std', sh, sW2) + sb2[:, None, :]
        shared = shared.mean(axis=0)
        gates = xf @ rW + rb
        topk_vals, topk_idx = jax.lax.top_k(gates, TOP_K)
        topk_probs = jax.nn.softmax(topk_vals, axis=-1)
        onehot = topk_idx[:, :, None] == jnp.arange(NUM_EXPERTS)[None, None, :]
        w = jnp.sum(topk_probs[:, :, None] * onehot, axis=1)
        h = _gelu(jnp.einsum('td,edh->eth', xf, W1) + b1[:, None, :])
        y = jnp.einsum('eth,ehd->etd', h, W2) + b2[:, None, :]
        moe = jnp.einsum('te,etd->td', w, y)
        return (shared + moe).reshape(B, L, D)
    x = x + _L0_xattn_ref(_layernorm(x, axis=-1), ctx_1024, L0_xattn_Wq, L0_xattn_bq, L0_xattn_Wk, L0_xattn_bk, L0_xattn_Wv, L0_xattn_bv, L0_xattn_Wo, L0_xattn_bo)
    x = x + _L0_attn_ref(_layernorm(x, axis=-1), L0_attn_Wk, L0_attn_Wv, L0_attn_Wq, L0_attn_Wp, L0_attn_bp)
    x = x + _L0_ffn_ref(_layernorm(x, axis=-1), L0_ffn_rW, L0_ffn_rb, L0_ffn_W1, L0_ffn_b1, L0_ffn_W2, L0_ffn_b2, L0_ffn_sW1, L0_ffn_sb1, L0_ffn_sW2, L0_ffn_sb2)
    return x

_drawn_inputs = setup_inputs


def setup_inputs(seed=0):
    import zlib

    import numpy as np

    out = dict(_drawn_inputs(seed))
    spreads = {'L0_xattn_bq': (0.0, 0.457),
     'L0_xattn_bk': (0.0, 2.0),
     'L0_xattn_bv': (0.0, 0.1),
     'L0_xattn_bo': (0.0, 0.1),
     'L0_attn_bp': (0.0, 0.1),
     'L0_ffn_rb': (0.0, 0.1),
     'L0_ffn_b1': (0.0, 0.1),
     'L0_ffn_b2': (0.0, 0.1),
     'L0_ffn_sb1': (0.0, 0.1),
     'L0_ffn_sb2': (0.0, 0.1)}
    factors = {'L0_attn_Wk': 8.0, 'L0_attn_Wq': 8.0}
    for name, (base, spread) in spreads.items():
        noise = np.random.default_rng([zlib.crc32(name.encode()), seed]).standard_normal(out[name].shape)
        drawn = base * np.exp(spread * noise) if base else spread * noise
        out[name] = jnp.asarray(drawn.astype(out[name].dtype))
    for name, factor in factors.items():
        out[name] = (out[name] * factor).astype(out[name].dtype)
    return out
```

```python
from contextlib import ExitStack

import concourse.bass as bass
from concourse import mybir

F32 = mybir.dt.float32
U32 = mybir.dt.uint32
I32 = mybir.dt.int32
ALU = mybir.AluOpType
ACT = mybir.ActivationFunctionType
AX = mybir.AxisListType

P = 128
D = 512
NB = 8
NQ = 64
SKV = 1601
PARTS = [(0, 384), (384, 384), (768, 384), (1152, 449)]
WID = 450
EPS = 1e-5
XSCALE = float(32) ** -0.5
ASCALE = float(512) ** -0.5
NE = 8
HID = 2048


class Engine:

    def __init__(self, name, sem):
        self.name, self.sem, self.n, self.ops, self.seen = name, sem, 0, [], {}

    def wait(self, *marks):
        for m in marks:
            if m is None:
                continue
            sem, value = m
            if self.seen.get(id(sem), 0) >= value:
                continue
            self.seen[id(sem)] = value
            self.ops.append(lambda e, sem=sem, value=value: e.wait_ge(sem, value))

    def do(self, fn):
        self.ops.append(fn)

    def mark(self, fn):
        self.n += 1
        sem = self.sem
        self.ops.append(lambda e: fn(e).then_inc(sem, 1))
        return (sem, self.n)

    def emit(self, e):
        for op in self.ops:
            op(e)


class Landing:

    def __init__(self, sem):
        self.sem, self.n = sem, 0

    def load(self, q, dst, src):
        self.n += 16
        sem = self.sem
        q.do(lambda e: e.dma_start(dst, src).then_inc(sem, 16))
        return (sem, self.n)


def build(nc, x, ctx0, ctx1, ctx2, ctx3, wq, bq, wk, bk, wv, bv, wo, bo, ak, av, aq, ap_, abp, rw, rb,
          w1, b1, w2, b2, out):
    ctxs = [ctx0, ctx1, ctx2, ctx3]
    st = ExitStack()
    with st:
        def sb(name, shape, dt=F32):
            return st.enter_context(nc.sbuf_tensor(name, shape, dt))

        def sem(name):
            return st.enter_context(nc.semaphore(name))

        PE, DVE, AC, PL, SP = (Engine(n, sem("done_" + n)) for n in ("pe", "dve", "act", "pool", "sp"))

        def landing(name):
            return Landing(sem("load_" + name))

        bank = [st.enter_context(nc.psum_tensor(f"bank{i}", [P, 512], F32)) for i in range(8)]
        sc2 = None

        ident = sb("ident", [P, P])
        mask = sb("mask", [P, 64])
        iota8 = sb("iota8", [P, 8])
        iota8i = sb("iota8i", [P, 8], I32)
        epsb = sb("epsb", [P, 1])
        xres = sb("xres", [P, 4, D])
        xn = sb("xn", [P, 4, D])
        xT = sb("xT", [P, 4, D])
        stats = sb("stats", [P, 4, 6])
        mv = sb("mv", [P, 4, 2])
        sd = sb("sd", [P, 4])
        rstd = sb("rstd", [P, 4])
        bqt = sb("bqt", [P, 4])
        bqs = sb("bqs", [P, 4])
        bkt = sb("bkt", [P, 4])
        bvt = sb("bvt", [P, 256])
        bot = sb("bot", [P, D])
        bpt = sb("bpt", [P, D])
        rbt = sb("rbt", [P, 8])
        rwt = sb("rwt", [P, 4, 8])
        b1t = sb("b1t", [P, 10, 16])
        b2t = sb("b2t", [10, D])
        akt = sb("akt", [P, 4, 64])
        avt = sb("avt", [P, 4, 128])

        wqt = sb("wqt", [P, 4, D])
        wkt = sb("wkt", [P, 4, D])
        wvt = sb("wvt", [P, 4, D])
        wot = sb("wot", [P, 4, D])
        aqt = wqt
        apt = sb("apt", [P, 4, D])
        qblk = sb("qblk", [P, 4, NB, 256])
        ctxt = sb("ctxt", [P, 2, 4 * WID])
        kT = sb("kT", [P, 2, 4, WID])
        vv = sb("vv", [P, 2, 4, 8, 66])
        tt = sb("tt", [P, 2, 1024])
        ss = sb("ss", [P, 2, 1024])
        rden = sb("rden", [P, 8])
        cc = sb("cc", [P, 8, 32])
        cT = sb("cT", [P, 2, 2, P])

        NR = 4
        ring = sb("ring", [P, NR, 2048])

        c_in = landing("in")
        m_x = c_in.load(SP, xres[:], x)
        c_wq = landing("wq")
        m_wq = c_wq.load(SP, wqt[:], wq)
        c_wk = landing("wk")
        m_wk = c_wk.load(SP, wkt[:], wk)
        c_ctx = [landing("ctx0"), landing("ctx1")]
        ctx_loaded = {}

        c_wv = landing("wv")
        c_sm = landing("small")
        m_sm = None

        def load_ctx(i):
            b, s = divmod(i, 4)
            n = PARTS[s][1]
            ctx_loaded[i] = c_ctx[i % 2].load(SP, ctxt[:, i % 2, 0:4 * n], ctxs[s][b])

        load_ctx(0)
        m_wv = c_wv.load(SP, wvt[:], wv)
        load_ctx(1)
        for dst, src in ((bqt, bq), (bkt, bk), (bvt, bv), (bot, bo), (bpt, abp), (rbt, rb), (rwt, rw),
                         (b1t, b1), (b2t, b2), (akt, ak), (avt, av)):
            m_sm = c_sm.load(SP, dst[:], src)
        c_wo = landing("wo")
        m_wo = c_wo.load(SP, wot[:], wo)
        c_aw = landing("aw")
        m_apt = c_aw.load(SP, apt[:], ap_)

        z = PL.mark(lambda e: e.memset(ident[:], 0.0))
        PL.wait(z)
        z = m_id = PL.mark(lambda e: e.affine_select(out=ident[:], in_=ident[:], compare_op=ALU.not_equal, fill=1.0,
                                                 base=0, pattern=[[-1, P]], channel_multiplier=1))
        PL.wait(z)
        z = PL.mark(lambda e: e.memset(mask[:], 0.0))
        PL.wait(z)
        z = PL.mark(lambda e: e.affine_select(out=mask[0:64, :], in_=mask[0:64, :], compare_op=ALU.is_ge, fill=-1e30,
                                          base=0, pattern=[[-1, 64]], channel_multiplier=1))
        PL.wait(z)
        m_mask = PL.mark(lambda e: e.affine_select(out=mask[64:128, :], in_=mask[64:128, :], compare_op=ALU.is_ge,
                                                   fill=-1e30, base=0, pattern=[[-1, 64]], channel_multiplier=1))
        PL.wait(m_mask)
        m_io = PL.mark(lambda e: e.iota(iota8i[:], pattern=[[1, 8]], base=0, channel_multiplier=0))
        PL.wait(m_io)
        m_q0 = PL.mark(lambda e: e.memset(qblk[:], 0.0))
        PL.wait(m_q0)
        m_v1 = PL.mark(lambda e: e.memset(vv[:], 1.0))
        m_eps = DVE.mark(lambda e: e.memset(epsb[:], EPS))
        DVE.wait(m_io)
        m_iota = DVE.mark(lambda e: e.tensor_copy(iota8[:], iota8i[:]))

        def layernorm(src, srcs_ready, ident_ready, banks, bank_free):
            for t in range(4):
                DVE.wait(srcs_ready[t])
                m = DVE.mark(lambda e, t=t: e.bn_stats(stats[:, t, :], src[:, t, :]))
            DVE.wait(m)
            for t in range(4):
                m = DVE.mark(lambda e, t=t: e.bn_aggr(mv[:, t, :], stats[:, t, :]))
            AC.wait(m, m_eps)
            m = AC.mark(lambda e: e.activation(sd[:], mv[:, :, 1], ACT.Sqrt, bias=epsb[:, 0:1]))
            DVE.wait(m)
            m = DVE.mark(lambda e: e.reciprocal(rstd[:], sd[:]))
            DVE.wait(m)
            ms = []
            for t in range(4):
                ms.append(DVE.mark(lambda e, t=t: e.tensor_scalar(xn[:, t, :], src[:, t, :], mv[:, t, 0:1],
                                                                  rstd[:, t:t + 1], ALU.subtract, ALU.mult)))
            PE.wait(ident_ready)
            done = []
            for c in range(4):
                PE.wait(bank_free[c])
                for t in range(4):
                    PE.wait(ms[t])
                    f = lambda e, c=c, t=t: e.transpose(banks[c][:, t * P:(t + 1) * P],
                                                        xn[:, t, c * P:(c + 1) * P], ident[:])
                    if t == 3:
                        m = PE.mark(f)
                    else:
                        PE.do(f)
                E = (AC, DVE)[c % 2]
                E.wait(m)
                if E is AC:
                    done.append(E.mark(lambda e, c=c: e.copy(xT[:, c, :], banks[c][:])))
                else:
                    done.append(E.mark(lambda e, c=c: e.tensor_copy(xT[:, c, :], banks[c][:])))
            return done, ms

        ln1, _ = layernorm(xres, [m_x] * 4, m_id, bank[0:4], [None] * 4)
        DVE.wait(m_sm)
        m_bqs = DVE.mark(lambda e: e.tensor_scalar(bqs[:], bqt[:], XSCALE, None, ALU.mult))
        AC.wait(m_bqs, m_q0)
        PE.wait(m_wq)
        q_done = []
        for g in range(4):
            bk_ = bank[4 + g]
            for c in range(4):
                PE.wait(ln1[c])
                f = lambda e, g=g, c=c, bk_=bk_: e.matmul(bk_[:], wqt[:, c, g * P:(g + 1) * P], xT[:, c, :],
                                                          start=(c == 0), stop=(c == 3))
                m = PE.mark(f) if c == 3 else PE.do(f)
            AC.wait(m)
            for h in range(4):
                r = slice(32 * h, 32 * h + 32)
                mq = AC.mark(lambda e, g=g, h=h, r=r, bk_=bk_: e.activation(
                    qblk[r, g, :, 64 * h:64 * h + 64], bk_[r, :].rearrange("p (b q) -> p b q", b=NB),
                    ACT.Identity, bias=bqs[r, g:g + 1], scale=XSCALE))
            q_done.append(mq)
        SP.wait(m)
        m_aw = c_aw.load(SP, aqt[:], aq)
        DVE.wait(m_sm)
        for t in range(4):
            m_xr = DVE.mark(lambda e, t=t: e.tensor_tensor(xres[:, t, :], xres[:, t, :], bot[:], ALU.add))

        pj = [bank[0], bank[1]]
        pj_free = [ln1[0], ln1[1]]
        pj_n = [0]
        scb = [(bank[2], bank[3]), (bank[4], bank[5])]
        sc_free = [[ln1[2], ln1[3]], [q_done[0], q_done[1]]]
        po = (bank[6], bank[7])
        po_free = [q_done[2], q_done[3]]
        ctx_free = [None, None]
        kT_free = [None, None]
        vv_free = [None, None]
        k_ready, v_ready = {}, {}
        t_free = [None, None]
        s_free = [None, None]

        def take_pj():
            i = pj_n[0] % 2
            pj_n[0] += 1
            return i

        def proj_steps(i):
            b, s = divmod(i, 4)
            n = PARTS[s][1]
            u = i % 2
            cv = ctxt[:, u, 0:4 * n].rearrange("p (c k) -> p c k", c=4)
            steps = []

            def kstep(g):
                def run():
                    j = take_pj()
                    PE.wait(pj_free[j], m_wk, ctx_loaded[i])
                    for c in range(4):
                        f = lambda e, c=c: e.matmul(pj[j][:, 0:n], wkt[:, c, g * P:(g + 1) * P], cv[:, c, :],
                                                    start=(c == 0), stop=(c == 3))
                        m = PE.mark(f) if c == 3 else PE.do(f)
                    AC.wait(m, kT_free[u], m_sm)
                    k_ready[i, g] = pj_free[j] = AC.mark(lambda e: e.activation(
                        kT[:, u, g, 0:n], pj[j][:, 0:n], ACT.Identity, bias=bkt[:, g:g + 1]))
                return run

            def vstep(k):
                kn = min(P, n - k * P)

                def run():
                    j = take_pj()
                    PE.wait(pj_free[j], m_wv, ctx_loaded[i])
                    for c in range(4):
                        f = lambda e, c=c: e.matmul(pj[j][0:kn, :], cv[:, c, k * P:k * P + kn], wvt[:, c, :],
                                                    start=(c == 0), stop=(c == 3))
                        m = PE.mark(f) if c == 3 else PE.do(f)
                    if k == (n + P - 1) // P - 1:
                        ctx_free[u] = m
                        if i + 2 < 4 * NB:
                            SP.wait(m)
                            load_ctx(i + 2)
                    AC.wait(m, vv_free[u], m_v1)
                    v_ready[i, k] = pj_free[j] = AC.mark(lambda e: e.copy(
                        vv[0:kn, u, k, :, 0:64], pj[j][0:kn, :].rearrange("p (a d) -> p a d", a=8)))
                return run

            return [kstep(g) for g in range(4)] + [vstep(k) for k in range((n + P - 1) // P)]

        chunks = [(b * 4 + s, k, min(P, PARTS[s][1] - k * P)) for b in range(NB) for s in range(4)
                  for k in range((PARTS[s][1] + P - 1) // P)]
        PER = len(chunks) // NB
        s_ready = {}

        def scores(n):
            i, k, kn = chunks[n]
            u, w, b = i % 2, n % 2, i // 4
            lo, hi = scb[w]
            PE.wait(*sc_free[w])
            for g in range(4):
                PE.wait(k_ready[i, g], q_done[g])
                tgt = (lo, hi)[g // 2][0:kn, 256 * (g % 2):256 * (g % 2) + 256]
                f = lambda e, g=g, tgt=tgt: e.matmul(tgt, kT[:, u, g, k * P:k * P + kn], qblk[:, g, b, :],
                                                     start=True, stop=True)
                m = PE.mark(f) if g % 2 else PE.do(f)
                if g % 2:
                    hb = g // 2
                    r = slice(512 * hb, 512 * hb + 512)
                    pb_ = (lo, hi)[hb]
                    DVE.wait(m, t_free[w] if hb == 0 else None)
                    mt = DVE.mark(lambda e, r=r, pb_=pb_: e.tensor_scalar(tt[0:kn, w, r], pb_[0:kn, :], -1.0, 0.0,
                                                                         ALU.mult, ALU.max))
            if k == (PARTS[i % 4][1] + P - 1) // P - 1:
                kT_free[u] = m
            AC.wait(mt)
            ml = AC.mark(lambda e: e.activation(tt[0:kn, w, :], tt[0:kn, w, :], ACT.Ln, bias=1.0))
            AC.wait(ml)
            me = AC.mark(lambda e: e.activation(tt[0:kn, w, :], tt[0:kn, w, :], ACT.Exp, scale=-1.0))
            return n, me

        def finish(n, me):
            i, k, kn = chunks[n]
            w = n % 2
            DVE.wait(me, s_free[w])
            for hb in range(2):
                r = slice(512 * hb, 512 * hb + 512)
                pb_ = scb[w][hb]
                mm = DVE.mark(lambda e, r=r, pb_=pb_: e.scalar_tensor_tensor(
                    ss[0:kn, w, r], pb_[0:kn, :], 0.0, tt[0:kn, w, r], ALU.max, ALU.add))
                sc_free[w][hb] = mm
            t_free[w] = mm
            s_ready[n] = mm

        def pv(n):
            i, k, kn = chunks[n]
            u, w = i % 2, n % 2
            first, last = n % PER == 0, n % PER == PER - 1
            PE.wait(s_ready[n], v_ready[i, k])
            if first:
                PE.wait(*po_free)
            for a in range(8):
                f = lambda e, a=a: e.matmul(po[a // 4][:, 66 * (a % 4):66 * (a % 4) + 66],
                                            ss[0:kn, w, 128 * a:128 * a + 128], vv[0:kn, u, k, a, :],
                                            start=(first and a % 4 == 0), stop=(last and a % 4 == 3),
                                            skip_group_check=True)
                m = PE.mark(f) if a == 7 else PE.do(f)
            s_free[w] = m
            if k == (PARTS[i % 4][1] + P - 1) // P - 1:
                vv_free[u] = m
            return m

        cT_free = [None]
        cc_free = [None]
        x2_ready = [None] * 4

        def batch_out(b, m):
            DVE.wait(m)
            o = [po[hb][:, 0:264].rearrange("p (a d) -> p a d", a=4) for hb in range(2)]
            for hb in range(2):
                mr = DVE.mark(lambda e, hb=hb: e.reciprocal(rden[:, 4 * hb:4 * hb + 4], o[hb][:, :, 64]))
            DVE.wait(mr, cc_free[0])
            for hb in range(2):
                for par in range(2):
                    r = slice(64 * par, 64 * par + 64)
                    mm = DVE.mark(lambda e, hb=hb, par=par, r=r: e.tensor_tensor(
                        cc[r, 4 * hb:4 * hb + 4, :], o[hb][r, :, 32 * par:32 * par + 32],
                        rden[r, 4 * hb:4 * hb + 4].unsqueeze(2).to_broadcast([64, 4, 32]), ALU.mult))
                po_free[hb] = mm
            DVE.wait(mm, m_sm)
            mc = DVE.mark(lambda e: e.tensor_tensor(cc[:], cc[:], bvt[:].rearrange("p (a d) -> p a d", a=8), ALU.add))

            def tail():
                j = take_pj()
                PE.wait(pj_free[j], mc, m_id)
                PE.do(lambda e: e.transpose(pj[j][:, 0:P], cc[:, 0:4, :], ident[:]))
                m = PE.mark(lambda e: e.transpose(pj[j][:, P:2 * P], cc[:, 4:8, :], ident[:]))
                cc_free[0] = m
                DVE.wait(m, cT_free[0] if b % 2 == 0 else None)
                q0 = 64 * (b % 2)
                m = pj_free[j] = DVE.mark(lambda e: e.tensor_copy(
                    cT[:, :, :, q0:q0 + 64],
                    pj[j][:, 0:256].rearrange("p (h r q) -> p h r q", h=2, r=2)))
                if b % 2:
                    t = b // 2
                    i2 = take_pj()
                    PE.wait(pj_free[i2], m, m_wo)
                    for kk in range(4):
                        f = lambda e, kk=kk: e.matmul(pj[i2][:], cT[:, kk // 2, kk % 2, :], wot[:, kk, :],
                                                      start=(kk == 0), stop=(kk == 3))
                        mo = PE.mark(f) if kk == 3 else PE.do(f)
                    cT_free[0] = mo
                    DVE.wait(mo, m_xr)
                    x2_ready[t] = pj_free[i2] = DVE.mark(lambda e: e.tensor_tensor(
                        xres[:, t, :], pj[i2][:], xres[:, t, :], ALU.add))
            return tail

        todo = []
        nparts = 4 * NB
        for st_ in proj_steps(0):
            st_()
        tail = None
        prev = None
        nn = 0
        for i in range(nparts):
            steps = proj_steps(i + 1) if i + 1 < nparts else []
            nk = (PARTS[i % 4][1] + P - 1) // P
            for k in range(nk):
                take = (len(steps) + nk - k - 1) // (nk - k)
                now = scores(nn)
                if prev is not None:
                    finish(*prev)
                for _ in range(take):
                    steps.pop(0)()
                if tail is not None and nn % PER == 2:
                    tail()
                    tail = None
                if prev is not None:
                    m = pv(prev[0])
                    if prev[0] % PER == PER - 1:
                        tail = batch_out(chunks[prev[0]][0] // 4, m)
                prev = now
                nn += 1
        finish(*prev)
        m = pv(prev[0])
        batch_out(NB - 1, m)()

        ln2, _ = layernorm(xres, x2_ready, m_id, bank[2:6], [sc_free[0][0], sc_free[0][1], sc_free[1][0], sc_free[1][1]])
        kflat = kT[:, :, :, :].rearrange("p a c k -> p (a c k)")
        K2 = kflat[0:64, 0:512]
        Q2 = qblk[0:64, 0:2, :, :].rearrange("p g b q -> p (g b q)")
        V2 = kflat[:, 512:1024].rearrange("p (t d) -> p t d", t=4)
        sm = ctxt[:, :, :].rearrange("p a k -> p (a k)")[:, 0:2048]
        pT = tt[:, :, :].rearrange("p a k -> p (a k)")
        oT = ss[:, :, :].rearrange("p a k -> p (a k)")
        mx = sb("mx", [P, 32])
        rs = sb("rs", [P, 32])
        PE.wait(m_aw, m_sm)
        last_pe = m
        PE.wait(pj_free[0])
        for c in range(4):
            PE.wait(ln2[c])
            f = lambda e, c=c: e.matmul(bank[0][0:64, :], akt[:, c, :], xT[:, c, :], start=(c == 0), stop=(c == 3))
            m = PE.mark(f) if c == 3 else PE.do(f)
        AC.wait(m)
        mk2 = AC.mark(lambda e: e.copy(K2, bank[0][0:64, :]))
        Q2v = Q2.rearrange("p (b h t) -> p b h t", h=8, b=8)
        bfree = {2: ln2[0], 3: ln2[1], 4: ln2[2], 5: ln2[3], 6: po_free[0], 7: po_free[1]}
        mq2 = [None] * 8
        for h in range(8):
            bi = 2 + h % 6
            PE.wait(bfree[bi])
            for c in range(4):
                f = lambda e, c=c, h=h, bi=bi: e.matmul(bank[bi][0:64, :], aqt[:, c, 64 * h:64 * h + 64], xT[:, c, :],
                                                        start=(c == 0), stop=(c == 3))
                m = PE.mark(f) if c == 3 else PE.do(f)
            E = (AC, DVE)[h % 2]
            E.wait(m)
            dst = Q2v[:, :, h, :]
            src = bank[bi][0:64, :].rearrange("p (b t) -> p b t", b=8)
            if E is AC:
                mq2[h] = bfree[bi] = E.mark(lambda e, dst=dst, src=src: e.copy(dst, src))
            else:
                mq2[h] = bfree[bi] = E.mark(lambda e, dst=dst, src=src: e.tensor_copy(dst, src))
        PE.wait(pj_free[1])
        for t in range(4):
            for c in range(4):
                f = lambda e, c=c, t=t: e.matmul(bank[1][:, 128 * t:128 * t + 128], xT[:, c, 128 * t:128 * t + 128],
                                                 avt[:, c, :], start=(c == 0), stop=(c == 3))
                m = PE.mark(f) if c == 3 else PE.do(f)
        AC.wait(m)
        mv2 = AC.mark(lambda e: e.copy(V2, bank[1][:].rearrange("p (t d) -> p t d", t=4)))
        for t in range(4):
            DVE.wait(m_sm)
            m_xr2 = None
        PE.wait(mk2, *mq2)
        msc = []
        for bp in range(4):
            bi = 2 + bp
            PE.wait(bfree[bi])
            for hp in range(4):
                for b2_ in range(2):
                    b = 2 * bp + b2_
                    o0 = (hp * 2 + b2_) * 64
                    f = lambda e, b=b, hp=hp, o0=o0, bi=bi: e.matmul(
                        bank[bi][:, o0:o0 + 64], Q2[:, 512 * b + 128 * hp:512 * b + 128 * hp + 128], K2[:, 64 * b:64 * b + 64],
                        start=True, stop=True)
                    m = PE.mark(f) if o0 == 448 else PE.do(f)
            msc.append(m)
        mp_ = []
        DVE.wait(m_mask)
        for bp in range(4):
            sl = sm[:, 512 * bp:512 * bp + 512].rearrange("p (a s) -> p a s", s=64)
            ps = bank[2 + bp][:].rearrange("p (a s) -> p a s", s=64)
            a8 = slice(8 * bp, 8 * bp + 8)
            DVE.wait(msc[bp])
            m = bfree[2 + bp] = DVE.mark(lambda e, sl=sl, ps=ps: e.scalar_tensor_tensor(
                sl, ps, ASCALE, mask[:].unsqueeze(1).to_broadcast([P, 8, 64]), ALU.mult, ALU.add))
            DVE.wait(m)
            m = DVE.mark(lambda e, sl=sl, a8=a8: e.tensor_reduce(mx[:, a8], sl, AX.X, ALU.max))
            DVE.wait(m)
            m = DVE.mark(lambda e, sl=sl, a8=a8: e.tensor_tensor(
                sl, sl, mx[:, a8].unsqueeze(2).to_broadcast([P, 8, 64]), ALU.subtract))
            AC.wait(m)
            mp_.append(AC.mark(lambda e, sl=sl: e.activation(sl, sl, ACT.Exp)))
        mn_ = []
        for bp in range(4):
            sl = sm[:, 512 * bp:512 * bp + 512].rearrange("p (a s) -> p a s", s=64)
            a8 = slice(8 * bp, 8 * bp + 8)
            DVE.wait(mp_[bp])
            m = DVE.mark(lambda e, sl=sl, a8=a8: e.tensor_reduce(rs[:, a8], sl, AX.X, ALU.add))
            DVE.wait(m)
            m = DVE.mark(lambda e, a8=a8: e.reciprocal(rs[:, a8], rs[:, a8]))
            DVE.wait(m)
            mn_.append(DVE.mark(lambda e, sl=sl, a8=a8: e.tensor_tensor(
                sl, sl, rs[:, a8].unsqueeze(2).to_broadcast([P, 8, 64]), ALU.mult)))
        mpt = []
        for bp in range(4):
            bi = 2 + bp
            PE.wait(bfree[bi], mn_[bp])
            for hp in range(4):
                f = lambda e, bp=bp, hp=hp, bi=bi: e.transpose(
                    bank[bi][:, 128 * hp:128 * hp + 128],
                    sm[:, 512 * bp + 128 * hp:512 * bp + 128 * hp + 128], ident[:])
                m = PE.mark(f) if hp == 3 else PE.do(f)
            AC.wait(m)
            mpt.append(AC.mark(lambda e, bp=bp, bi=bi: e.copy(pT[:, 512 * bp:512 * bp + 512], bank[bi][:])))
            bfree[bi] = mpt[-1]
        oTv = oT.rearrange("p (h k) -> p h k", h=4)
        PE.wait(mv2)
        bfree[0], bfree[1] = mk2, mv2
        mo_ = []
        for b in range(8):
            bi = (6, 7, 0, 1)[b % 4]
            r = slice(64 * (b % 2), 64 * (b % 2) + 64)
            PE.wait(bfree[bi], mpt[b // 2])
            m = PE.mark(lambda e, b=b, bi=bi, r=r: e.matmul(
                bank[bi][:], V2[r, b // 2, :], pT[r, 512 * (b // 2):512 * (b // 2) + 512], start=True, stop=True))
            E = (DVE, AC)[b % 2]
            E.wait(m)
            pv4 = bank[bi][:].rearrange("p (h x t) -> p h x t", h=4, x=2)
            for h2 in range(2):
                q = slice(64 * h2, 64 * h2 + 64)
                dst, src = oTv[q, :, 64 * b:64 * b + 64], pv4[q, :, h2, :]
                if E is AC:
                    m = E.mark(lambda e, dst=dst, src=src: e.copy(dst, src))
                else:
                    m = E.mark(lambda e, dst=dst, src=src: e.tensor_copy(dst, src))
            bfree[bi] = m
            mo_.append(m)
        x3_ready = []
        for t in range(4):
            m = DVE.mark(lambda e, t=t: e.tensor_tensor(xres[:, t, :], xres[:, t, :], bpt[:], ALU.add))
        DVE.wait(m)
        for t in range(4):
            bi = 2 + t
            PE.wait(bfree[bi], mo_[2 * t], mo_[2 * t + 1])
            for hp in range(4):
                f = lambda e, t=t, hp=hp, bi=bi: e.matmul(bank[bi][:], oTv[:, hp, 128 * t:128 * t + 128],
                                                          apt[:, hp, :], start=(hp == 0), stop=(hp == 3))
                m = PE.mark(f) if hp == 3 else PE.do(f)
            DVE.wait(m)
            m = DVE.mark(lambda e, t=t, bi=bi: e.tensor_tensor(xres[:, t, :], bank[bi][:], xres[:, t, :], ALU.add))
            bfree[bi] = m
            x3_ready.append(m)

        ln3, _ = layernorm(xres, x3_ready, m_id, bank[0:4], [bfree[i] for i in range(4)])
        gates = sb("gates", [P, 4, 8])
        top = sb("top", [P, 4, 8])
        tidx = sb("tidx", [P, 4, 8], U32)
        tif = sb("tif", [P, 4, 8])
        pr = sb("pr", [P, 4, 4])
        wts = sb("wts", [P, 4, 10])
        wtm = sb("wtm", [P, 4, 8])
        wT = kflat[0:10, 1024:1536]
        PE.wait(bfree[4])
        for t in range(4):
            for c in range(4):
                PE.wait(ln3[c])
                f = lambda e, t=t, c=c: e.matmul(bank[4][:, 8 * t:8 * t + 8], xT[:, c, 128 * t:128 * t + 128],
                                                 rwt[:, c, :], start=(c == 0), stop=(c == 3))
                m = PE.mark(f) if c == 3 else PE.do(f)
        DVE.wait(m)
        m = DVE.mark(lambda e: e.tensor_tensor(gates[:], bank[4][:, 0:32].rearrange("p (t e) -> p t e", t=4),
                                               rbt[:].unsqueeze(1).to_broadcast([P, 4, 8]), ALU.add))
        bfree[4] = m
        DVE.wait(m)
        for t in range(4):
            m = DVE.mark(lambda e, t=t: e.max(top[:, t, :], gates[:, t, :]))
        DVE.wait(m)
        for t in range(4):
            m = DVE.mark(lambda e, t=t: e.max_index(tidx[:, t, :], top[:, t, :], gates[:, t, :]))
        DVE.wait(m)
        DVE.do(lambda e: e.tensor_copy(tif[:], tidx[:]))
        m = DVE.mark(lambda e: e.tensor_tensor(pr[:, :, 0], top[:, :, 1], top[:, :, 0], ALU.subtract))
        AC.wait(m)
        m = AC.mark(lambda e: e.activation(pr[:, :, 1], pr[:, :, 0], ACT.Exp))
        DVE.wait(m)
        m = DVE.mark(lambda e: e.tensor_scalar(pr[:, :, 2], pr[:, :, 1], 1.0, None, ALU.add))
        DVE.wait(m)
        m = DVE.mark(lambda e: e.reciprocal(pr[:, :, 2], pr[:, :, 2]))
        DVE.wait(m)
        m = DVE.mark(lambda e: e.tensor_tensor(pr[:, :, 3], pr[:, :, 2], pr[:, :, 1], ALU.mult))
        m0 = DVE.mark(lambda e: e.memset(wts[:], 0.5))
        DVE.wait(m, m0)
        for t in range(4):
            DVE.mark(lambda e, t=t: e.tensor_scalar(wts[:, t, 0:8], iota8[:], tif[:, t, 0:1], pr[:, t, 2:3],
                                                    ALU.is_equal, ALU.mult))
            m = DVE.mark(lambda e, t=t: e.tensor_scalar(wtm[:, t, :], iota8[:], tif[:, t, 1:2], pr[:, t, 3:4],
                                                        ALU.is_equal, ALU.mult))
        DVE.wait(m)
        m_w = DVE.mark(lambda e: e.tensor_tensor(wts[:, :, 0:8], wts[:, :, 0:8], wtm[:], ALU.add))
        PE.wait(m_w, bfree[5])
        for t in range(4):
            f = lambda e, t=t: e.transpose(bank[5][0:10, 128 * t:128 * t + 128], wts[:, t, :], ident[:])
            m = PE.mark(f) if t == 3 else PE.do(f)
        AC.wait(m)
        m_wT = bfree[5] = AC.mark(lambda e: e.copy(wT, bank[5][0:10, :]))

        hT = qblk[:, :, :, :].rearrange("p g b q -> p (g b q)").rearrange("p (j t) -> p j t", j=16)
        ring_land = [landing(f"ring{i}") for i in range(NR)]
        ring_free = [None] * NR
        units = [(e, kind, q) for e in range(10) for q in range(4) for kind in (0, 1)]
        loaded = {}

        def load_unit(n):
            e, kind, q = units[n]
            s = n % NR
            SP.wait(ring_free[s])
            src = (w1, w2)[kind][e, q]
            loaded[units[n]] = (s, ring_land[s].load(SP, ring[:, s, :], src))

        for n in range(NR):
            load_unit(n)
        nload = [NR]

        def unit_done(m):
            n = nload[0]
            s = n % NR
            ring_free[s] = m
            if n < len(units):
                load_unit(n)
            nload[0] += 1

        hfree = [ln3[0], ln3[1], ln3[2], ln3[3]]
        yfree = [bfree[4], bfree[5], bfree[6], bfree[7]]
        for t in range(4):
            PE.wait(yfree[t], m_wT)
            m = PE.mark(lambda e, t=t: e.matmul(bank[4 + t][:], wT[:, 128 * t:128 * t + 128], b2t[:],
                                                start=True, stop=True))
            DVE.wait(m)
            yfree[t] = acc_m = DVE.mark(lambda e, t=t: e.tensor_tensor(xres[:, t, :], bank[4 + t][:], xres[:, t, :],
                                                                       ALU.add))
        h_done = {}
        hT_free = {}
        AC.wait(m_aw)

        def hid(e_, j):
            q, jj = divmod(j, 4)
            s, ml = loaded[e_, 0, q]
            b_ = j % 4
            PE.wait(hfree[b_], ml)
            wv_ = ring[:, s, :].rearrange("p (c h) -> p c h", c=4)
            for c in range(4):
                f = lambda e, c=c: e.matmul(bank[b_][:], wv_[:, c, 128 * jj:128 * jj + 128], xT[:, c, :],
                                            start=(c == 0), stop=(c == 3))
                m = PE.mark(f) if c == 3 else PE.do(f)
            if jj == 3:
                unit_done(m)
            AC.wait(m, hT_free.get(j))
            h_done[e_, j] = hfree[b_] = AC.mark(lambda e: e.activation(hT[:, j, :], bank[b_][:], ACT.Gelu,
                                                                      bias=b1t[:, e_, j:j + 1]))

        def down(e_, j):
            q, jj = divmod(j, 4)
            s, ml = loaded[e_, 1, q]
            PE.wait(ml, h_done[e_, j])
            wv_ = ring[:, s, :].rearrange("p (c h) -> p c h", c=4)
            for t in range(4):
                if j == 0:
                    PE.wait(yfree[t])
                f = lambda e, t=t: e.matmul(bank[4 + t][:], hT[:, j, 128 * t:128 * t + 128], wv_[:, jj, :],
                                            start=(j == 0), stop=(j == 15))
                m = PE.mark(f) if (t == 3 or j == 15) else PE.do(f)
                if j == 15:
                    DVE.wait(m, acc_m)
                    yfree[t] = DVE.mark(lambda e, t=t: e.scalar_tensor_tensor(
                        xres[:, t, :], bank[4 + t][:], wts[:, t, e_:e_ + 1], xres[:, t, :], ALU.mult, ALU.add))
            hT_free[j] = m
            if jj == 3:
                unit_done(m)

        order = [(e_, j) for e_ in range(10) for j in range(16)]
        LAG = 3
        for n in range(len(order) + LAG):
            if n < len(order):
                hid(*order[n])
            if n >= LAG:
                if n - LAG > 0 and order[n - LAG][1] == 0:
                    for t in range(4):
                        DVE.wait(yfree[t])
                down(*order[n - LAG])
        c_out = landing("out")
        for t in range(4):
            SP.wait(yfree[t])
            mo = c_out.load(SP, out[t], xres[:, t, :])
        SP.wait(mo)

        block = st.enter_context(nc.Block())
        block.tensor(PE.emit)
        block.vector(DVE.emit)
        block.scalar(AC.emit)
        block.gpsimd(PL.emit)
        block.sync(SP.emit)


def kernel(**inputs):
    import numpy as np
    import concourse.bacc as bacc
    from concourse.bass_utils import run_bass_kernel_spmd as run

    a = {k: np.asarray(v) for k, v in inputs.items()}
    c = np.ascontiguousarray

    def rows(w):
        return c(w.reshape(4, P, -1).transpose(1, 0, 2))

    def spread(v):
        return c(np.broadcast_to(v.reshape(1, -1), (P, v.size)))

    ctxT = a["ctx_1024"].transpose(0, 2, 1).reshape(NB, 4, P, SKV).transpose(0, 2, 1, 3)
    arrays = {"x": c(a["x"].reshape(4, P, D).transpose(1, 0, 2))}
    for i, (k0, n) in enumerate(PARTS):
        arrays[f"ctx{i}"] = c(ctxT[:, :, :, k0:k0 + n]).reshape(NB, P, 4 * n)
    arrays["wq"] = rows(a["L0_xattn_Wq"].T)
    arrays["bq"] = c(a["L0_xattn_bq"].reshape(4, P).T)
    arrays["wk"] = rows(a["L0_xattn_Wk"].T)
    arrays["bk"] = c(a["L0_xattn_bk"].reshape(4, P).T)
    arrays["wv"] = rows(a["L0_xattn_Wv"].T)
    bv = a["L0_xattn_bv"].reshape(8, 2, 32).transpose(1, 0, 2).reshape(2, 1, 256)
    arrays["bv"] = c(np.broadcast_to(bv, (2, 64, 256)).reshape(P, 256))
    wo = a["L0_xattn_Wo"].T.reshape(2, 4, 2, 32, D).transpose(0, 2, 1, 3, 4).reshape(4, P, D)
    arrays["wo"] = c(wo.transpose(1, 0, 2))
    arrays["bo"] = spread(a["L0_xattn_bo"])
    arrays["ak"] = rows(a["L0_attn_Wk"])
    arrays["av"] = rows(np.concatenate([a["L0_attn_Wv"]] * 2, axis=1))
    arrays["aq"] = rows(a["L0_attn_Wq"].transpose(1, 0, 2).reshape(D, D))
    arrays["ap_"] = rows(a["L0_attn_Wp"])
    arrays["abp"] = spread(a["L0_attn_bp"])
    arrays["rw"] = rows(a["L0_ffn_rW"])
    arrays["rb"] = spread(a["L0_ffn_rb"])
    w1 = np.concatenate([a["L0_ffn_W1"], a["L0_ffn_sW1"]])
    arrays["w1"] = c(w1.reshape(10, 4, P, 4, 512).transpose(0, 3, 2, 1, 4)).reshape(10, 4, P, 2048)
    b1 = np.concatenate([a["L0_ffn_b1"], a["L0_ffn_sb1"]])
    arrays["b1"] = c(b1.reshape(10, 16, P).transpose(2, 0, 1))
    w2 = np.concatenate([a["L0_ffn_W2"], a["L0_ffn_sW2"]])
    arrays["w2"] = c(w2.reshape(10, 4, 4, P, 512).transpose(0, 1, 3, 2, 4)).reshape(10, 4, P, 2048)
    arrays["b2"] = c(np.concatenate([a["L0_ffn_b2"], a["L0_ffn_sb2"]]))

    nc = bacc.Bacc("TRN2", target_bir_lowering=False, num_devices=1)
    args = {k: nc.dram_tensor("in_" + k, v.shape, mybir.dt.from_np(v.dtype), kind="ExternalInput").ap()
            for k, v in arrays.items()}
    o = nc.dram_tensor("out_0", (4, P, D), F32, kind="ExternalOutput").ap()
    build(nc, out=o, **args)
    r = run(nc, [{"in_" + k: v for k, v in arrays.items()}], core_ids=[0])
    return r.results[0]["out_0"].reshape(NB, NQ, D)
```

```python
from contextlib import ExitStack

import concourse.bass as bass
from concourse import mybir

F32 = mybir.dt.float32
F32R = mybir.dt.float32r
BF16 = mybir.dt.bfloat16
U32 = mybir.dt.uint32
I32 = mybir.dt.int32
ALU = mybir.AluOpType
ACT = mybir.ActivationFunctionType
AX = mybir.AxisListType

P = 128
D = 512
NB = 8
NQ = 64
SKV = 1601
PARTS = [(0, 384), (384, 384), (768, 384), (1152, 449)]
WID = 450
EPS = 1e-5
XSCALE = float(32) ** -0.5
ASCALE = float(512) ** -0.5
NE = 8
HID = 2048


class Engine:

    def __init__(self, name, sem):
        self.name, self.sem, self.n, self.ops, self.seen = name, sem, 0, [], {}

    def wait(self, *marks):
        for m in marks:
            if m is None:
                continue
            sem, value = m
            if self.seen.get(id(sem), 0) >= value:
                continue
            self.seen[id(sem)] = value
            self.ops.append(lambda e, sem=sem, value=value: e.wait_ge(sem, value))

    def do(self, fn):
        self.ops.append(fn)

    def mark(self, fn):
        self.n += 1
        sem = self.sem
        self.ops.append(lambda e: fn(e).then_inc(sem, 1))
        return (sem, self.n)

    def when(self, cond):
        self.outer = self.ops
        self.ops = []
        self.outer.append((cond, self.ops))

    def always(self):
        self.ops = self.outer

    def emit(self, e, ops=None):
        for op in self.ops if ops is None else ops:
            if isinstance(op, tuple):
                with e.If(op[0]()):
                    self.emit(e, op[1])
            else:
                op(e)


class Landing:

    def __init__(self, sem):
        self.sem, self.n = sem, 0

    def load(self, q, dst, src):
        self.n += 16
        sem = self.sem
        q.do(lambda e: e.dma_start(dst, src).then_inc(sem, 16))
        return (sem, self.n)


def build(nc, x, ctx0, ctx1, ctx2, ctx3, wq, bq, wk, bk, wv, bv, wo, bo, ak, av, aq, ap_, abp, rw, rb,
          w1, b1, w2, b2, out):
    ctxs = [ctx0, ctx1, ctx2, ctx3]
    st = ExitStack()
    with st:
        def sb(name, shape, dt=F32):
            return st.enter_context(nc.sbuf_tensor(name, shape, dt))

        def sem(name):
            return st.enter_context(nc.semaphore(name))

        PE, DVE, AC, PL, SP = (Engine(n, sem("done_" + n)) for n in ("pe", "dve", "act", "pool", "sp"))

        def landing(name):
            return Landing(sem("load_" + name))

        bank = [st.enter_context(nc.psum_tensor(f"bank{i}", [P, 512], F32)) for i in range(8)]
        sc2 = None

        NR = 9
        ident = sb("ident", [P, P])
        mask = sb("mask", [P, 64])
        iota8 = sb("iota8", [P, 8])
        iotai = sb("iotai", [P, 256], I32)
        epsb = sb("epsb", [P, 1])
        xres = sb("xres", [P, 4, D])
        xn = sb("xn", [P, 4, D])
        xT = sb("xT", [P, 4, D])
        stats = sb("stats", [P, 4, 6])
        mv = sb("mv", [P, 4, 2])
        sd = sb("sd", [P, 4])
        rstd = sb("rstd", [P, 4])
        bqt = sb("bqt", [P, 4])
        bqs = sb("bqs", [P, 4])
        bkt = sb("bkt", [P, 4])
        bvt = sb("bvt", [P, 4, 64])
        bot = sb("bot", [P, D])
        bpt = sb("bpt", [P, D])
        rbt = sb("rbt", [P, 8])
        rwt = sb("rwt", [P, 4, 8])
        b1s = sb("b1s", [P, 2, 16])
        iota128 = sb("iota128", [P, P])
        kio = sb("kio", [P, 15, 8])
        tri = sb("tri", [P, P], BF16)
        ones = sb("ones", [P, P], BF16)
        b2t = sb("b2t", [10, D])
        akt = sb("akt", [P, 4, 64])
        avt = sb("avt", [P, 4, 128])

        part1 = ExitStack()

        def sb1(name, shape, dt=F32):
            return part1.enter_context(nc.sbuf_tensor(name, shape, dt))

        wkh = sb1("wkh", [P, 4, D], F32R)
        wkl = sb1("wkl", [P, 4, D], F32R)
        wvh = sb1("wvh", [P, 4, D], F32R)
        wvl = sb1("wvl", [P, 4, D], F32R)
        cxh = sb1("cxh", [P, 2, 4, WID], F32R)
        cxl = sb1("cxl", [P, 2, 4, WID], F32R)
        ctxt = sb1("ctxt", [P, 2, 4 * WID])
        kT = sb1("kT", [P, 2, 4, WID])
        vv = sb1("vv", [P, 2, 4, D])
        wqt = sb1("wqt", [P, 4, D])
        wot = wqt
        qblk = sb1("qblk", [P, 4, NB, 256])
        tt = sb1("tt", [P, 2, 1024])
        ss = sb1("ss", [P, 2, 1024])
        sel = sb1("sel", [P, 4, P])
        wkt = ss[:, :, :].rearrange("p a (c n) -> p (a c) n", c=2)
        wvt = tt[:, :, :].rearrange("p a (c n) -> p (a c) n", c=2)
        dacc = xn[:, :, :].rearrange("p (a c) n -> p a (c n)", a=2)
        cU = xT[:, 0, :].rearrange("p (a g q) -> p a g q", a=2, g=4)
        rden = xT[:, 1, 0:256]
        cT = xT[:, 2, :].rearrange("p (g q) -> p g q", g=4)

        c_in = landing("in")
        m_x = c_in.load(SP, xres[:], x)
        c_wq = landing("wq")
        m_wq = c_wq.load(SP, wqt[:], wq)
        c_wk = landing("wk")
        m_wk = c_wk.load(SP, wkt[:], wk)
        c_ctx = [landing("ctx0"), landing("ctx1")]
        ctx_loaded = {}

        c_wv = landing("wv")
        c_sm = landing("small")
        m_sm = None

        def load_ctx(i):
            b, s = divmod(i, 4)
            n = PARTS[s][1]
            ctx_loaded[i] = c_ctx[i % 2].load(SP, ctxt[:, i % 2, 0:4 * n], ctxs[s][b])

        load_ctx(0)
        m_wv = c_wv.load(SP, wvt[:], wv)
        load_ctx(1)
        for dst, src in ((bqt, bq), (bkt, bk), (bvt, bv), (bot, bo), (bpt, abp), (rbt, rb), (rwt, rw),
                         (b1s[:, 0, :], b1[8]), (b1s[:, 1, :], b1[9]), (b2t, b2), (akt, ak), (avt, av)):
            m_sm = c_sm.load(SP, dst[:] if hasattr(dst, "name") else dst, src)
        c_wo = landing("wo")
        c_aw = landing("aw")

        z = PL.mark(lambda e: e.memset(ident[:], 0.0))
        PL.wait(z)
        z = m_id = PL.mark(lambda e: e.affine_select(out=ident[:], in_=ident[:], compare_op=ALU.not_equal, fill=1.0,
                                                 base=0, pattern=[[-1, P]], channel_multiplier=1))
        PL.wait(z)
        z = PL.mark(lambda e: e.memset(mask[:], 0.0))
        PL.wait(z)
        z = PL.mark(lambda e: e.affine_select(out=mask[0:64, :], in_=mask[0:64, :], compare_op=ALU.is_ge, fill=-1e30,
                                          base=0, pattern=[[-1, 64]], channel_multiplier=1))
        PL.wait(z)
        m_mask = PL.mark(lambda e: e.affine_select(out=mask[64:128, :], in_=mask[64:128, :], compare_op=ALU.is_ge,
                                                   fill=-1e30, base=0, pattern=[[-1, 64]], channel_multiplier=1))
        PL.wait(m_mask)
        z = PL.mark(lambda e: e.memset(ones[:], 1.0))
        PL.wait(z)
        z = PL.mark(lambda e: e.memset(tri[:], 1.0))
        PL.wait(z)
        z = PL.mark(lambda e: e.affine_select(out=tri[:], in_=tri[:], compare_op=ALU.is_ge, fill=0.0,
                                              base=-1, pattern=[[1, P]], channel_multiplier=-1))
        PL.wait(z)
        z = PL.mark(lambda e: e.iota(iotai[:, 0:P], pattern=[[1, P]], base=0, channel_multiplier=0))
        PL.wait(z)
        m_io = PL.mark(lambda e: e.iota(iotai[:, P:P + 120], pattern=[[1, 15], [0, 8]], base=0, channel_multiplier=0))
        PL.wait(m_io)
        m_q0 = PL.mark(lambda e: e.memset(qblk[:], 0.0))
        PL.wait(m_q0)
        PL.wait(m_q0)
        z = PL.mark(lambda e: e.memset(sel[:], 0.0))
        for h in range(4):
            PL.wait(z)
            z = m_sel = PL.mark(lambda e, h=h: e.memset(sel[:, h, 32 * h:32 * h + 32], 1.0))
        for t_ in (cxh, cxl):
            for u in range(2):
                m_pad = DVE.mark(lambda e, t_=t_, u=u: e.memset(t_[:, u, :, 449:450].bitcast(F32), 0.0))
        m_eps = DVE.mark(lambda e: e.memset(epsb[:], EPS))
        DVE.wait(m_io)
        DVE.do(lambda e: e.tensor_copy(iota8[:], iotai[:, 0:8]))
        DVE.do(lambda e: e.tensor_copy(iota128[:], iotai[:, 0:P]))
        m_iota = DVE.mark(lambda e: e.tensor_copy(kio[:], iotai[:, P:P + 120].rearrange("p (k e) -> p k e", e=8)))

        def layernorm(src, srcs_ready, ident_ready, banks, bank_free):
            for t in range(4):
                DVE.wait(srcs_ready[t])
                m = DVE.mark(lambda e, t=t: e.bn_stats(stats[:, t, :], src[:, t, :]))
            DVE.wait(m)
            for t in range(4):
                m = DVE.mark(lambda e, t=t: e.bn_aggr(mv[:, t, :], stats[:, t, :]))
            AC.wait(m, m_eps)
            m = AC.mark(lambda e: e.activation(sd[:], mv[:, :, 1], ACT.Sqrt, bias=epsb[:, 0:1]))
            DVE.wait(m)
            m = DVE.mark(lambda e: e.reciprocal(rstd[:], sd[:]))
            DVE.wait(m)
            ms = []
            for t in range(4):
                ms.append(DVE.mark(lambda e, t=t: e.tensor_scalar(xn[:, t, :], src[:, t, :], mv[:, t, 0:1],
                                                                  rstd[:, t:t + 1], ALU.subtract, ALU.mult)))
            PE.wait(ident_ready)
            done = []
            for c in range(4):
                PE.wait(bank_free[c])
                for t in range(4):
                    PE.wait(ms[t])
                    f = lambda e, c=c, t=t: e.transpose(banks[c][:, t * P:(t + 1) * P],
                                                        xn[:, t, c * P:(c + 1) * P], ident[:])
                    if t == 3:
                        m = PE.mark(f)
                    else:
                        PE.do(f)
                E = (AC, DVE)[c % 2]
                E.wait(m)
                if E is AC:
                    done.append(E.mark(lambda e, c=c: e.copy(xT[:, c, :], banks[c][:])))
                else:
                    done.append(E.mark(lambda e, c=c: e.tensor_copy(xT[:, c, :], banks[c][:])))
            return done, ms

        ln1, _ = layernorm(xres, [m_x] * 4, m_id, bank[0:4], [None] * 4)
        DVE.wait(m_sm)
        m_bqs = DVE.mark(lambda e: e.tensor_scalar(bqs[:], bqt[:], XSCALE, None, ALU.mult))
        AC.wait(m_bqs, m_q0)
        PE.wait(m_wq)
        q_done = []
        for g in range(4):
            bk_ = bank[4 + g]
            for c in range(4):
                PE.wait(ln1[c])
                f = lambda e, g=g, c=c, bk_=bk_: e.matmul(bk_[:], wqt[:, c, g * P:(g + 1) * P], xT[:, c, :],
                                                          start=(c == 0), stop=(c == 3))
                m = PE.mark(f) if c == 3 else PE.do(f)
            AC.wait(m)
            for h in range(4):
                r = slice(32 * h, 32 * h + 32)
                mq = AC.mark(lambda e, g=g, h=h, r=r, bk_=bk_: e.activation(
                    qblk[r, g, :, 64 * h:64 * h + 64], bk_[r, :].rearrange("p (b q) -> p b q", b=NB),
                    ACT.Identity, bias=bqs[r, g:g + 1], scale=XSCALE))
            q_done.append(mq)
        SP.wait(m)
        m_wo = c_wo.load(SP, wot[:], wo)
        DVE.wait(m_sm)
        for t in range(4):
            m_xr = DVE.mark(lambda e, t=t: e.tensor_tensor(xres[:, t, :], xres[:, t, :], bot[:], ALU.add))

        def split(hi, lo, src, ready, E_lo):
            AC.wait(*ready)
            mh = AC.mark(lambda e: e.copy(hi, src))
            E_lo.wait(*ready, mh)
            ml_ = E_lo.mark(lambda e: e.tensor_tensor(lo, src, hi.bitcast(F32), ALU.subtract))
            return mh, ml_

        _, m_wks = split(wkh[:], wkl[:], wkt, [m_wk], DVE)
        _, m_wvs = split(wvh[:], wvl[:], wvt, [m_wv], DVE)
        AC.do(lambda e: e.preload_act_table_set("natural_log_exp_and_others"))
        cx_ready = {}
        cx_free = [None, None]

        def split_ctx(i):
            s, u = i % 4, i % 2
            n = PARTS[s][1]
            src = ctxt[:, u, 0:4 * n].rearrange("p (c k) -> p c k", c=4)
            mh, ml_ = split(cxh[:, u, :, 0:n], cxl[:, u, :, 0:n], src,
                            [ctx_loaded[i], cx_free[u], m_pad], PL)
            cx_ready[i] = (mh, ml_)
            if i + 2 < 4 * NB:
                SP.wait(ml_)
                load_ctx(i + 2)

        pj = [bank[0], bank[1]]
        pj_free = [ln1[0], ln1[1]]
        pj_n = [0]
        scb = [(bank[2], bank[3]), (bank[4], bank[5])]
        sc_free = [[ln1[2], ln1[3]], [q_done[0], q_done[1]]]
        po = (bank[6], bank[7])
        po_free = [q_done[2], q_done[3]]
        kT_free = [None, None]
        vv_free = [None, None]
        k_ready, v_ready = {}, {}
        t_free = [None, None]
        sd_free = [None, None]
        dacc_m = [None]
        dacc_free = [ln1[3], ln1[3]]
        s_free = [None, None]

        def take_pj():
            i = pj_n[0] % 2
            pj_n[0] += 1
            return i

        def proj_steps(i):
            b, s = divmod(i, 4)
            n = PARTS[s][1]
            u = i % 2
            nn_ = n + n % 2
            three = lambda h, l: ((h, 0), (h, 1), (l, 0))
            steps = []

            def kstep(g):
                def run():
                    j = take_pj()
                    PE.wait(pj_free[j], m_wks, *cx_ready[i])
                    for c in range(4):
                        for x_, (w_, lo_) in enumerate(three(wkh, wkl)):
                            mv_ = (cxh, cxl)[lo_]
                            f = lambda e, c=c, w_=w_, mv_=mv_, x_=x_: e.matmul(
                                pj[j][:, 0:nn_], w_[:, c, g * P:(g + 1) * P], mv_[:, u, c, 0:nn_],
                                start=(c == 0 and x_ == 0), stop=(c == 3 and x_ == 2))
                            m = PE.mark(f) if (c == 3 and x_ == 2) else PE.do(f)
                    AC.wait(m, kT_free[u], m_sm)
                    k_ready[i, g] = pj_free[j] = AC.mark(lambda e: e.activation(
                        kT[:, u, g, 0:n], pj[j][:, 0:n], ACT.Identity, bias=bkt[:, g:g + 1]))
                return run

            def vstep(k):
                kn = min(P, n - k * P)

                def run():
                    j = take_pj()
                    PE.wait(pj_free[j], m_wvs, *cx_ready[i])
                    for c in range(4):
                        for x_, (w_, lo_) in enumerate(three(cxh, cxl)):
                            mv_ = (wvh, wvl)[lo_]
                            f = lambda e, c=c, w_=w_, mv_=mv_, x_=x_: e.matmul(
                                pj[j][0:kn, :], w_[:, u, c, k * P:k * P + kn], mv_[:, c, :],
                                start=(c == 0 and x_ == 0), stop=(c == 3 and x_ == 2))
                            m = PE.mark(f) if (c == 3 and x_ == 2) else PE.do(f)
                    if k == (n + P - 1) // P - 1:
                        cx_free[u] = m
                    AC.wait(m, vv_free[u])
                    v_ready[i, k] = pj_free[j] = AC.mark(lambda e: e.copy(vv[0:kn, u, k, :], pj[j][0:kn, :]))
                return run

            return [kstep(g) for g in range(4)] + [vstep(k) for k in range((n + P - 1) // P)]

        chunks = [(b * 4 + s, k, min(P, PARTS[s][1] - k * P)) for b in range(NB) for s in range(4)
                  for k in range((PARTS[s][1] + P - 1) // P)]
        PER = len(chunks) // NB
        s_ready = {}

        def scores(n):
            i, k, kn = chunks[n]
            u, w, b = i % 2, n % 2, i // 4
            lo, hi = scb[w]
            PE.wait(*sc_free[w])
            for g in range(4):
                PE.wait(k_ready[i, g], q_done[g])
                tgt = (lo, hi)[g // 2][0:kn, 256 * (g % 2):256 * (g % 2) + 256]
                f = lambda e, g=g, tgt=tgt: e.matmul(tgt, kT[:, u, g, k * P:k * P + kn], qblk[:, g, b, :],
                                                     start=True, stop=True)
                m = PE.mark(f) if g % 2 else PE.do(f)
                if g % 2:
                    hb = g // 2
                    r = slice(512 * hb, 512 * hb + 512)
                    pb_ = (lo, hi)[hb]
                    DVE.wait(m, t_free[w] if hb == 0 else None)
                    mt = DVE.mark(lambda e, r=r, pb_=pb_: e.tensor_scalar(tt[0:kn, w, r], pb_[0:kn, :], -1.0, 0.0,
                                                                         ALU.mult, ALU.max))
            if k == (PARTS[i % 4][1] + P - 1) // P - 1:
                kT_free[u] = m
            AC.wait(mt)
            ml = AC.mark(lambda e: e.activation(tt[0:kn, w, :], tt[0:kn, w, :], ACT.Ln, bias=1.0))
            AC.wait(ml)
            me = AC.mark(lambda e: e.activation(tt[0:kn, w, :], tt[0:kn, w, :], ACT.Exp, scale=-1.0))
            return n, me

        def finish(n, me):
            i, k, kn = chunks[n]
            w = n % 2
            DVE.wait(me, s_free[w], sd_free[w])
            for hb in range(2):
                r = slice(512 * hb, 512 * hb + 512)
                pb_ = scb[w][hb]
                mm = DVE.mark(lambda e, r=r, pb_=pb_: e.scalar_tensor_tensor(
                    ss[0:kn, w, r], pb_[0:kn, :], 0.0, tt[0:kn, w, r], ALU.max, ALU.add))
                sc_free[w][hb] = mm
            t_free[w] = mm
            s_ready[n] = mm

        def pv(n):
            i, k, kn = chunks[n]
            u, w = i % 2, n % 2
            first, last = n % PER == 0, n % PER == PER - 1
            PE.wait(s_ready[n], v_ready[i, k])
            if first:
                PE.wait(*po_free)
            for g in range(4):
                f = lambda e, g=g: e.matmul(po[g // 2][:, 256 * (g % 2):256 * (g % 2) + 256],
                                            vv[0:kn, u, k, g * P:(g + 1) * P], ss[0:kn, w, 256 * g:256 * g + 256],
                                            start=(first and g % 2 == 0), stop=(last and g % 2 == 1),
                                            skip_group_check=True)
                m = PE.mark(f) if g == 3 else PE.do(f)
            s_free[w] = m
            y = (n // PER) % 2
            PL.wait(s_ready[n], dacc_m[0])
            if first:
                PL.wait(dacc_free[y])
                dacc_m[0] = PL.mark(lambda e: e.tensor_copy(dacc[0:kn, y, :], ss[0:kn, w, :]))
            else:
                dacc_m[0] = PL.mark(lambda e: e.tensor_tensor(dacc[0:kn, y, :], dacc[0:kn, y, :], ss[0:kn, w, :],
                                                              ALU.add))
            sd_free[w] = dacc_m[0]
            if k == (PARTS[i % 4][1] + P - 1) // P - 1:
                vv_free[u] = m
            return m

        cT_free = [None]
        cU_free = [None, None]
        x2_ready = [None] * 4

        def batch_out(b, m):
            y = b % 2
            md = dacc_m[0]
            for hb, E in ((0, DVE), (1, AC)):
                E.wait(m, cU_free[y])
                src = po[hb][:, :].rearrange("p (g h q) -> p g h q", g=2, h=4)
                for h in range(4):
                    r = slice(32 * h, 32 * h + 32)
                    cp = (lambda e, o, i_: e.copy(o, i_)) if E is AC else (lambda e, o, i_: e.tensor_copy(o, i_))
                    f = lambda e, cp=cp, r=r, h=h, src=src, hb=hb: cp(e, cU[r, y, 2 * hb:2 * hb + 2, :],
                                                                      src[r, :, h, :])
                    mm = E.mark(f)
                po_free[hb] = mm

            def tail():
                j = take_pj()
                PE.wait(pj_free[j], md, m_sel)
                dv = dacc[:, y, :].rearrange("p (g h q) -> p g h q", g=4, h=4)
                for h in range(4):
                    f = lambda e, h=h: e.matmul(pj[j][:, 0:256], sel[:, h, :], dv[:, :, h, :],
                                                start=(h == 0), stop=(h == 3))
                    m = PE.mark(f) if h == 3 else PE.do(f)
                dacc_free[y] = m
                DVE.wait(m, cT_free[0] if y == 0 else None)
                pj_free[j] = m = DVE.mark(lambda e: e.reciprocal(rden, pj[j][:, 0:256]))
                DVE.wait(m, *po_free_of)
                m = DVE.mark(lambda e: e.tensor_tensor(cU[:, y, :, :], cU[:, y, :, :],
                                                       rden.rearrange("p (g q) -> p g q", g=4), ALU.mult))
                DVE.wait(m, m_sm)
                m = DVE.mark(lambda e: e.tensor_tensor(cT[:, :, 64 * y:64 * y + 64], cU[:, y, :, :], bvt[:],
                                                       ALU.add))
                cU_free[y] = m
                return m

            def tail2(m):
                if b % 2:
                    t = b // 2
                    i2 = take_pj()
                    PE.wait(pj_free[i2], m, m_wo)
                    for kk in range(4):
                        f = lambda e, kk=kk: e.matmul(pj[i2][:], cT[:, kk, :], wot[:, kk, :],
                                                      start=(kk == 0), stop=(kk == 3))
                        mo = PE.mark(f) if kk == 3 else PE.do(f)
                    cT_free[0] = mo
                    DVE.wait(mo, m_xr)
                    x2_ready[t] = pj_free[i2] = DVE.mark(lambda e: e.tensor_tensor(
                        xres[:, t, :], pj[i2][:], xres[:, t, :], ALU.add))
            po_free_of = list(po_free)
            tail = (tail, tail2)
            return tail

        nparts = 4 * NB
        split_ctx(0)
        split_ctx(1)
        for st_ in proj_steps(0):
            st_()
        tail = mt_ = None
        prev = None
        nn = 0
        for i in range(nparts):
            steps = proj_steps(i + 1) if i + 1 < nparts else []
            nk = (PARTS[i % 4][1] + P - 1) // P
            for k in range(nk):
                take = (len(steps) + nk - k - 1) // (nk - k)
                now = scores(nn)
                if k == 1 and i + 2 < nparts:
                    split_ctx(i + 2)
                if prev is not None:
                    finish(*prev)
                for _ in range(take):
                    steps.pop(0)()
                if tail is not None and nn % PER == 2:
                    mt_ = tail[0]()
                if tail is not None and nn % PER == 4:
                    tail[1](mt_)
                    tail = None
                if prev is not None:
                    m = pv(prev[0])
                    if prev[0] % PER == PER - 1:
                        tail = batch_out(chunks[prev[0]][0] // 4, m)
                prev = now
                nn += 1
        finish(*prev)
        m = pv(prev[0])
        tail = batch_out(NB - 1, m)
        tail[1](tail[0]())
        part1.close()
        NBLK = 15
        regs = {}
        p1_end = x2_ready[3]

        ln2, _ = layernorm(xres, x2_ready, m_id, bank[2:6], [sc_free[0][0], sc_free[0][1], sc_free[1][0], sc_free[1][1]])
        ring = sb("ring", [P, NR, 2048])
        ring_land = [landing(f"ring{i}") for i in range(NR)]
        ring_free = {}
        units = [("s", e, q, kind) for e in (8, 9) for q in range(4) for kind in (0, 1)]
        units += [("r", k, q, kind) for k in range(NBLK) for kind in (0, 1) for q in range(4)]
        number = {u: n for n, u in enumerate(units)}
        loaded = {}

        def load_unit(u):
            n = number[u]
            what, k, q, kind = u
            SP.wait(ring_free[units[n - NR]] if n >= NR else p1_end)
            src = (w1, w2)[kind]
            land = ring_land[n % NR]
            if what == "s":
                loaded[u] = land.load(SP, ring[:, n % NR, :], src[k, q])
            else:
                land.n += 16
                SP.do(lambda e: e.dma_start(ring[:, n % NR, :], src[regs["e", k], q]).then_inc(land.sem, 16))
                loaded[u] = (land.sem, land.n)

        part2 = ExitStack()

        def sb2(name, shape, dt=F32):
            return part2.enter_context(nc.sbuf_tensor(name, shape, dt))

        aqt = sb2("aqt", [P, 4, D])
        apt = sb2("apt", [P, 4, D])
        K2 = sb2("K2", [64, D])[:]
        Q2 = sb2("Q2", [64, 4096])[:]
        V2 = sb2("V2", [P, 4, P])[:]
        sm = sb2("sm", [P, 2048])[:]
        pT = sb2("pT", [P, 2048])[:]
        oT = sb2("oT", [P, 2048])[:]
        SP.wait(p1_end)
        c_aw.load(SP, aqt[:], aq)
        m_aw = c_aw.load(SP, apt[:], ap_)
        for u in units[:NR]:
            load_unit(u)
        mx = sb2("mx", [P, 32])
        rs = sb2("rs", [P, 32])
        PE.wait(m_aw, m_sm)
        last_pe = m
        PE.wait(pj_free[0])
        for c in range(4):
            PE.wait(ln2[c])
            f = lambda e, c=c: e.matmul(bank[0][0:64, :], akt[:, c, :], xT[:, c, :], start=(c == 0), stop=(c == 3))
            m = PE.mark(f) if c == 3 else PE.do(f)
        AC.wait(m)
        mk2 = AC.mark(lambda e: e.copy(K2, bank[0][0:64, :]))
        Q2v = Q2.rearrange("p (b h t) -> p b h t", h=8, b=8)
        bfree = {2: ln2[0], 3: ln2[1], 4: ln2[2], 5: ln2[3], 6: po_free[0], 7: po_free[1]}
        mq2 = [None] * 8
        for h in range(8):
            bi = 2 + h % 6
            PE.wait(bfree[bi])
            for c in range(4):
                f = lambda e, c=c, h=h, bi=bi: e.matmul(bank[bi][0:64, :], aqt[:, c, 64 * h:64 * h + 64], xT[:, c, :],
                                                        start=(c == 0), stop=(c == 3))
                m = PE.mark(f) if c == 3 else PE.do(f)
            E = (AC, DVE)[h % 2]
            E.wait(m)
            dst = Q2v[:, :, h, :]
            src = bank[bi][0:64, :].rearrange("p (b t) -> p b t", b=8)
            if E is AC:
                mq2[h] = bfree[bi] = E.mark(lambda e, dst=dst, src=src: e.copy(dst, src))
            else:
                mq2[h] = bfree[bi] = E.mark(lambda e, dst=dst, src=src: e.tensor_copy(dst, src))
        PE.wait(pj_free[1])
        for t in range(4):
            for c in range(4):
                f = lambda e, c=c, t=t: e.matmul(bank[1][:, 128 * t:128 * t + 128], xT[:, c, 128 * t:128 * t + 128],
                                                 avt[:, c, :], start=(c == 0), stop=(c == 3))
                m = PE.mark(f) if c == 3 else PE.do(f)
        AC.wait(m)
        mv2 = AC.mark(lambda e: e.copy(V2, bank[1][:].rearrange("p (t d) -> p t d", t=4)))
        for t in range(4):
            DVE.wait(m_sm)
            m_xr2 = None
        PE.wait(mk2, *mq2)
        msc = []
        for bp in range(4):
            bi = 2 + bp
            PE.wait(bfree[bi])
            for hp in range(4):
                for b2_ in range(2):
                    b = 2 * bp + b2_
                    o0 = (hp * 2 + b2_) * 64
                    f = lambda e, b=b, hp=hp, o0=o0, bi=bi: e.matmul(
                        bank[bi][:, o0:o0 + 64], Q2[:, 512 * b + 128 * hp:512 * b + 128 * hp + 128], K2[:, 64 * b:64 * b + 64],
                        start=True, stop=True)
                    m = PE.mark(f) if o0 == 448 else PE.do(f)
            msc.append(m)
        mp_ = []
        DVE.wait(m_mask)
        for bp in range(4):
            sl = sm[:, 512 * bp:512 * bp + 512].rearrange("p (a s) -> p a s", s=64)
            ps = bank[2 + bp][:].rearrange("p (a s) -> p a s", s=64)
            a8 = slice(8 * bp, 8 * bp + 8)
            DVE.wait(msc[bp])
            m = bfree[2 + bp] = DVE.mark(lambda e, sl=sl, ps=ps: e.scalar_tensor_tensor(
                sl, ps, ASCALE, mask[:].unsqueeze(1).to_broadcast([P, 8, 64]), ALU.mult, ALU.add))
            DVE.wait(m)
            m = DVE.mark(lambda e, sl=sl, a8=a8: e.tensor_reduce(mx[:, a8], sl, AX.X, ALU.max))
            DVE.wait(m)
            m = DVE.mark(lambda e, sl=sl, a8=a8: e.tensor_tensor(
                sl, sl, mx[:, a8].unsqueeze(2).to_broadcast([P, 8, 64]), ALU.subtract))
            AC.wait(m)
            mp_.append(AC.mark(lambda e, sl=sl: e.activation(sl, sl, ACT.Exp)))
        mn_ = []
        for bp in range(4):
            sl = sm[:, 512 * bp:512 * bp + 512].rearrange("p (a s) -> p a s", s=64)
            a8 = slice(8 * bp, 8 * bp + 8)
            DVE.wait(mp_[bp])
            m = DVE.mark(lambda e, sl=sl, a8=a8: e.tensor_reduce(rs[:, a8], sl, AX.X, ALU.add))
            DVE.wait(m)
            m = DVE.mark(lambda e, a8=a8: e.reciprocal(rs[:, a8], rs[:, a8]))
            DVE.wait(m)
            mn_.append(DVE.mark(lambda e, sl=sl, a8=a8: e.tensor_tensor(
                sl, sl, rs[:, a8].unsqueeze(2).to_broadcast([P, 8, 64]), ALU.mult)))
        mpt = []
        for bp in range(4):
            bi = 2 + bp
            PE.wait(bfree[bi], mn_[bp])
            for hp in range(4):
                f = lambda e, bp=bp, hp=hp, bi=bi: e.transpose(
                    bank[bi][:, 128 * hp:128 * hp + 128],
                    sm[:, 512 * bp + 128 * hp:512 * bp + 128 * hp + 128], ident[:])
                m = PE.mark(f) if hp == 3 else PE.do(f)
            AC.wait(m)
            mpt.append(AC.mark(lambda e, bp=bp, bi=bi: e.copy(pT[:, 512 * bp:512 * bp + 512], bank[bi][:])))
            bfree[bi] = mpt[-1]
        oTv = oT.rearrange("p (h k) -> p h k", h=4)
        PE.wait(mv2)
        bfree[0], bfree[1] = mk2, mv2
        mo_ = []
        for b in range(8):
            bi = (6, 7, 0, 1)[b % 4]
            r = slice(64 * (b % 2), 64 * (b % 2) + 64)
            PE.wait(bfree[bi], mpt[b // 2])
            m = PE.mark(lambda e, b=b, bi=bi, r=r: e.matmul(
                bank[bi][:], V2[r, b // 2, :], pT[r, 512 * (b // 2):512 * (b // 2) + 512], start=True, stop=True))
            E = (DVE, AC)[b % 2]
            E.wait(m)
            pv4 = bank[bi][:].rearrange("p (h x t) -> p h x t", h=4, x=2)
            for h2 in range(2):
                q = slice(64 * h2, 64 * h2 + 64)
                dst, src = oTv[q, :, 64 * b:64 * b + 64], pv4[q, :, h2, :]
                if E is AC:
                    m = E.mark(lambda e, dst=dst, src=src: e.copy(dst, src))
                else:
                    m = E.mark(lambda e, dst=dst, src=src: e.tensor_copy(dst, src))
            bfree[bi] = m
            mo_.append(m)
        x3_ready = []
        for t in range(4):
            m = DVE.mark(lambda e, t=t: e.tensor_tensor(xres[:, t, :], xres[:, t, :], bpt[:], ALU.add))
        DVE.wait(m)
        for t in range(4):
            bi = 2 + t
            PE.wait(bfree[bi], mo_[2 * t], mo_[2 * t + 1])
            for hp in range(4):
                f = lambda e, t=t, hp=hp, bi=bi: e.matmul(bank[bi][:], oTv[:, hp, 128 * t:128 * t + 128],
                                                          apt[:, hp, :], start=(hp == 0), stop=(hp == 3))
                m = PE.mark(f) if hp == 3 else PE.do(f)
            DVE.wait(m)
            m = DVE.mark(lambda e, t=t, bi=bi: e.tensor_tensor(xres[:, t, :], bank[bi][:], xres[:, t, :], ALU.add))
            bfree[bi] = m
            x3_ready.append(m)

        p2_end = x3_ready[3]
        ln3, _ = layernorm(xres, x3_ready, m_id, bank[0:4], [bfree[i] for i in range(4)])
        part2.close()
        wT = sb("wT", [10, 512])
        G = sb("G", [P, 2, 4, P])
        GA = xT[:, 0, :].rearrange("p (t k) -> p t k", t=4)
        GB = xT[:, 1, :].rearrange("p (t k) -> p t k", t=4)
        GwT = xT[:, 2:4, :].rearrange("p a (t k) -> p a t k", t=4)
        xg = sb("xg", [P, 2, 4, P])
        b1r = sb("b1r", [P, NBLK, 16])
        gates = sb("gates", [P, 4, 8])
        top = sb("top", [P, 4, 8])
        tidx = sb("tidx", [P, 4, 8], U32)
        tif = sb("tif", [P, 4, 8])
        pr = sb("pr", [P, 4, 4])
        wts = sb("wts", [P, 4, 10])
        oh = sb("oh", [P, 2, 4, 8])
        ohw = sb("ohw", [P, 2, 4, 8])
        sel8 = sb("sel8", [P, 4, 8], BF16)
        cnt = sb("cnt", [P, 8])
        nbk = sb("nbk", [P, 2, 8])
        ends = sb("ends", [P, 3, 8])
        base = sb("base", [P, 8])
        gsl = sb("gsl", [P, 4, 8])
        gse = sb("gse", [P, 2, 4, 8])
        gs = sb("gs", [P, 2, 4])
        gsk = sb("gsk", [P, 2, 2, 4])
        kcmp = sb("kcmp", [P, 15, 8])
        kexp = sb("kexp", [P, 16])
        kint = sb("kint", [P, 16], I32)
        part3 = ExitStack()

        def sb3(name, shape, dt=F32):
            return part3.enter_context(nc.sbuf_tensor(name, shape, dt))

        xTh = sb3("xTh", [P, 4, D], F32R)
        xTl = sb3("xTl", [P, 4, D], F32R)
        wsh = sb3("wsh", [P, 3, 2048], F32R)
        wsl = sb3("wsl", [P, 3, 2048], F32R)
        hr = sb3("hr", [P, 2, D])
        hh = sb3("hh", [P, 4, D], F32R)
        hl = sb3("hl", [P, 4, D], F32R)

        ws_ready, ws_free = {}, {}

        def split_unit(n):
            if n >= 16:
                return
            u = units[n]
            x_ = n % 3
            ready = [loaded[u], p2_end] + ([ws_free[n - 3]] if n >= 3 else [])
            mh, ml_ = split(wsh[:, x_, :], wsl[:, x_, :], ring[:, n % NR, :], ready, DVE)
            ws_ready[n] = (mh, ml_)
            ring_free[u] = ml_
            if units[n + NR][0] == "s":
                load_unit(units[n + NR])

        x_split = []
        for c in range(4):
            AC.wait(ln3[c])
            mh = AC.mark(lambda e, c=c: e.copy(xTh[:, c, :], xT[:, c, :]))
            DVE.wait(mh, ln3[c])
            x_split += [mh, DVE.mark(lambda e, c=c: e.tensor_tensor(xTl[:, c, :], xT[:, c, :],
                                                                    xTh[:, c, :].bitcast(F32), ALU.subtract))]
        PE.wait(ln3[2])
        for t in range(4):
            for c in range(4):
                PE.wait(ln3[c])
                f = lambda e, t=t, c=c: e.matmul(bank[2][:, 8 * t:8 * t + 8], xT[:, c, 128 * t:128 * t + 128],
                                                 rwt[:, c, :], start=(c == 0), stop=(c == 3))
                m = PE.mark(f) if c == 3 else PE.do(f)
        m_gates = m
        split_unit(0)
        split_unit(1)

        def dve(fn, *waits):
            DVE.wait(chain[0], *waits)
            chain[0] = DVE.mark(fn)
            return chain[0]

        chain = [None]

        def route1():
            b_free2 = dve(lambda e: e.tensor_tensor(gates[:], bank[2][:, 0:32].rearrange("p (t e) -> p t e", t=4),
                                                    rbt[:].unsqueeze(1).to_broadcast([P, 4, 8]), ALU.add), m_gates)
            for t in range(4):
                dve(lambda e, t=t: e.max(top[:, t, :], gates[:, t, :]))
            for t in range(4):
                dve(lambda e, t=t: e.max_index(tidx[:, t, :], top[:, t, :], gates[:, t, :]))
            m = dve(lambda e: e.tensor_tensor(pr[:, :, 0], top[:, :, 1], top[:, :, 0], ALU.subtract))
            AC.wait(m)
            me = AC.mark(lambda e: e.activation(pr[:, :, 1], pr[:, :, 0], ACT.Exp))
            dve(lambda e: e.tensor_copy(tif[:], tidx[:]))
            for n_ in range(2):
                dve(lambda e, n_=n_: e.tensor_tensor(oh[:, n_, :, :], iota8[:].unsqueeze(1).to_broadcast([P, 4, 8]),
                                                     tif[:, :, n_:n_ + 1].to_broadcast([P, 4, 8]), ALU.is_equal))
            m_sel8 = dve(lambda e: e.tensor_tensor(sel8[:], oh[:, 0, :, :], oh[:, 1, :, :], ALU.add))
            dve(lambda e: e.tensor_scalar(pr[:, :, 2], pr[:, :, 1], 1.0, None, ALU.add), me)
            dve(lambda e: e.reciprocal(pr[:, :, 2], pr[:, :, 2]))
            dve(lambda e: e.tensor_tensor(pr[:, :, 3], pr[:, :, 2], pr[:, :, 1], ALU.mult))
            for n_ in range(2):
                dve(lambda e, n_=n_: e.tensor_tensor(ohw[:, n_, :, :], oh[:, n_, :, :],
                                                     pr[:, :, 2 + n_:3 + n_].to_broadcast([P, 4, 8]), ALU.mult))
            dve(lambda e: e.memset(wts[:], 0.5))
            m_w = dve(lambda e: e.tensor_tensor(wts[:, :, 0:8], ohw[:, 0, :, :], ohw[:, 1, :, :], ALU.add))
            PE.wait(m_sel8, b_free2, m_io)
            for t in range(4):
                for t_ in range(t + 1):
                    f = lambda e, t=t, t_=t_: e.matmul(bank[2][:, 8 * t:8 * t + 8], (tri if t_ == t else ones)[:],
                                                       sel8[:, t_, :], start=(t_ == 0), stop=(t_ == t))
                    PE.do(f)
            for t_ in range(4):
                f = lambda e, t_=t_: e.matmul(bank[2][:, 32:40], ones[:], sel8[:, t_, :], start=(t_ == 0),
                                              stop=(t_ == 3))
                m_pos = PE.mark(f) if t_ == 3 else PE.do(f)
            return m_pos, m_w

        def route2(m_pos, m_w):
            PE.wait(m_w, ln3[3])
            for t in range(4):
                f = lambda e, t=t: e.transpose(bank[3][0:10, 128 * t:128 * t + 128], wts[:, t, :], ident[:])
                m = PE.mark(f) if t == 3 else PE.do(f)
            AC.wait(m)
            m_wT = AC.mark(lambda e: e.copy(wT[:], bank[3][0:10, :]))
            dve(lambda e: e.tensor_copy(cnt[:], bank[2][:, 32:40]), m_pos)
            dve(lambda e: e.tensor_scalar(nbk[:, 0, :], cnt[:], 0.0, None, ALU.is_gt))
            for n_ in range(3):
                dve(lambda e, n_=n_: e.scalar_tensor_tensor(nbk[:, (n_ + 1) % 2, :], cnt[:], 128.0 * (n_ + 1),
                                                            nbk[:, n_ % 2, :], ALU.is_gt, ALU.add))
            src = nbk[:, 1, :]
            for n_, d in enumerate((1, 2, 4)):
                dve(lambda e, n_=n_, d=d, src=src: e.tensor_copy(ends[:, n_, 0:d], src[:, 0:d]))
                dve(lambda e, n_=n_, d=d, src=src: e.tensor_tensor(ends[:, n_, d:8], src[:, d:8], src[:, 0:8 - d],
                                                                   ALU.add))
                src = ends[:, n_, :]
            end = ends[:, 2, :]
            dve(lambda e: e.tensor_tensor(kcmp[:], kio[:], end.unsqueeze(1).to_broadcast([P, 15, 8]), ALU.is_ge))
            dve(lambda e: e.tensor_reduce(kexp[:, 0:15], kcmp[:], AX.X, ALU.add))
            dve(lambda e: e.tensor_scalar(kexp[:, 0:15], kexp[:, 0:15], 7.0, None, ALU.min))
            dve(lambda e: e.tensor_copy(kexp[:, 15:16], end[:, 7:8]))
            m_int = dve(lambda e: e.tensor_copy(kint[:], kexp[:]))
            dve(lambda e: e.tensor_tensor(base[:], end, nbk[:, 1, :], ALU.subtract))
            m_b2 = dve(lambda e: e.scalar_tensor_tensor(gsl[:], base[:].unsqueeze(1).to_broadcast([P, 4, 8]), 128.0,
                                                        bank[2][:, 0:32].rearrange("p (t e) -> p t e", t=4),
                                                        ALU.mult, ALU.add))
            dve(lambda e: e.tensor_tensor(gse[:], oh[:], gsl[:].unsqueeze(1).to_broadcast([P, 2, 4, 8]), ALU.mult))
            dve(lambda e: e.tensor_reduce(gs[:], gse[:], AX.X, ALU.add))
            for E in (SP, PE, AC, DVE):
                E.wait(m_int)
                E.do(lambda e, E=E: regs.__setitem__(("n", E.name), e.value_load(kint[0:1, 15:16], min_val=0,
                                                                               max_val=NBLK)))
            return m_wT, m_b2

        bank3_free = [None]
        G_free = [None, None]
        xg_ready, gwt_ready = {}, {}
        xg_free, gwt_free = [None, None], [None, None]
        g_marks = {}

        def build_G(k):
            y = k % 2
            dve(lambda e: e.tensor_scalar(gsk[:, y, :, :], gs[:], -128.0 * k, None, ALU.add))
            io = iota128[:].unsqueeze(1).to_broadcast([P, 4, P])
            for n_, X in ((0, GA), (1, GB)):
                dve(lambda e, n_=n_, X=X: e.tensor_tensor(X, io, gsk[:, y, n_, :].unsqueeze(2).to_broadcast(
                    [P, 4, P]), ALU.is_equal), gw_used[0])
            mg = dve(lambda e: e.tensor_tensor(G[:, y, :, :], GA, GB, ALU.add), G_free[y])
            for n_, X in ((0, GA), (1, GB)):
                dve(lambda e, n_=n_, X=X: e.tensor_tensor(X, X, pr[:, :, 2 + n_:3 + n_].to_broadcast(
                    [P, 4, P]), ALU.mult))
            mw = dve(lambda e: e.tensor_tensor(GA, GA, GB, ALU.add))
            g_marks[k] = (mg, mw)

        gw_used = [m_gates]

        def gather(k):
            y = k % 2
            mg, mw = g_marks[k]
            PE.wait(mg, bank3_free[0])
            for c in range(4):
                for t in range(4):
                    f = lambda e, c=c, t=t: e.matmul(bank[3][:, P * c:P * c + P], xn[:, t, P * c:P * c + P],
                                                     G[:, y, t, :], start=(t == 0), stop=(t == 3))
                    m = PE.mark(f) if (c == 3 and t == 3) else PE.do(f)
            G_free[y] = m
            DVE.wait(m, xg_free[y])
            xg_ready[k] = bank3_free[0] = DVE.mark(lambda e: e.tensor_copy(
                xg[:, y, :, :], bank[3][:].rearrange("p (c k) -> p c k", c=4)))

        def turn(k):
            y = k % 2
            PE.wait(g_marks[k][1], bank3_free[0])
            for t in range(4):
                f = lambda e, t=t: e.transpose(bank[3][:, P * t:P * t + P], GA[:, t, :], ident[:])
                m = PE.mark(f) if t == 3 else PE.do(f)
            gw_used[0] = m
            AC.wait(m, gwt_free[y])
            gwt_ready[k] = bank3_free[0] = AC.mark(lambda e: e.copy(
                GwT[:, y, :, :], bank[3][:].rearrange("p (c k) -> p c k", c=4)))

        def load_block(k):
            if k >= NE:
                SP.when(lambda k=k: regs["n", "sp"] > k)
            SP.do(lambda e: regs.__setitem__(("e", k), e.value_load(kint[0:1, k:k + 1], min_val=0, max_val=7)))
            m = b1_land[k]
            SP.do(lambda e: e.dma_start(b1r[:, k, :], b1[regs["e", k]]).then_inc(m.sem, 16))
            for kind in (0, 1):
                for q in range(4):
                    load_unit(("r", k, q, kind))
            if k >= NE:
                SP.always()

        b1_land = [landing(f"b1_{k}") for k in range(NBLK)]

        hfree = [ln3[0], ln3[1]]
        h_done, hb_free = {}, {}
        order = [(e_, j) for e_ in range(2) for j in range(16)]

        def hid(n):
            e_, j = order[n]
            q, jj = divmod(j, 4)
            un = number["s", 8 + e_, q, 0]
            b_, r_ = n % 2, n % 4
            PE.wait(hfree[b_], *ws_ready[un], *x_split)
            k_ = 0
            for c in range(4):
                for w_, x_ in ((wsh, xTh), (wsh, xTl), (wsl, xTh)):
                    f = lambda e, c=c, w_=w_, x_=x_, k_=k_: e.matmul(
                        bank[b_][:], w_[:, un % 3, 512 * c + 128 * jj:512 * c + 128 * jj + 128], x_[:, c, :],
                        start=(k_ == 0), stop=(k_ == 11))
                    m = PE.mark(f) if k_ == 11 else PE.do(f)
                    k_ += 1
            if jj == 3:
                ws_free[un] = m
            AC.wait(m, h_done.get(n - 2))
            hfree[b_] = mg = AC.mark(lambda e: e.activation(hr[:, n % 2, :], bank[b_][:], ACT.Gelu,
                                                            bias=b1s[:, e_, j:j + 1]))
            DVE.wait(mg, hb_free.get(n - 4))
            mh = DVE.mark(lambda e: e.tensor_copy(hh[:, r_, :], hr[:, n % 2, :]))
            DVE.wait(mh)
            h_done[n] = DVE.mark(lambda e: e.tensor_tensor(hl[:, r_, :], hr[:, n % 2, :], hh[:, r_, :].bitcast(F32),
                                                           ALU.subtract))
            return un if jj == 3 else None

        def down(n):
            e_, j = order[n]
            q, jj = divmod(j, 4)
            un = number["s", 8 + e_, q, 1]
            r_ = n % 4
            PE.wait(*ws_ready[un], h_done[n])
            if n == 0:
                PE.wait(*[bfree[i] for i in range(4, 8)])
            for t in range(4):
                for k_, (h_, w_) in enumerate(((hh, wsh), (hh, wsl), (hl, wsh))):
                    f = lambda e, t=t, k_=k_, h_=h_, w_=w_: e.matmul(
                        bank[4 + t][:], h_[:, r_, P * t:P * t + P], w_[:, un % 3, 512 * jj:512 * jj + 512],
                        start=(n == 0 and k_ == 0), stop=(n == 31 and k_ == 2))
                    m = PE.mark(f) if k_ == 2 else PE.do(f)
                if n == 31:
                    y_done.append(m)
            hb_free[n] = m
            if jj == 3:
                ws_free[un] = m
            return un if jj == 3 else None

        y_done = []
        split_unit(2)
        m_pos, m_w = route1()
        nsplit = 3
        LAG = 3
        for n in range(32 + LAG):
            d1 = hid(n) if n < 32 else None
            if n == 1:
                m_wT, m_b2 = route2(m_pos, m_w)
                load_block_at = True
            if n == 3:
                build_G(0)
            if n == 6:
                bank3_free[0] = m_wT
                gather(0)
                turn(0)
            if d1 is not None and nsplit - 3 in ws_free:
                split_unit(nsplit)
                nsplit += 1
            d2 = down(n - LAG) if n >= LAG else None
            while nsplit < 16 and nsplit - 3 in ws_free:
                split_unit(nsplit)
                nsplit += 1
        xr_done = []
        for t in range(4):
            DVE.wait(y_done[t])
            xr_done.append(DVE.mark(lambda e, t=t: e.scalar_tensor_tensor(xres[:, t, :], bank[4 + t][:], 0.5,
                                                                          xres[:, t, :], ALU.mult, ALU.add)))
            PE.wait(xr_done[t], m_wT)
            PE.do(lambda e, t=t: e.matmul(bank[4 + t][:], wT[:, P * t:P * t + P], b2t[:], start=True, stop=True,
                                          skip_group_check=True))
        part3.close()
        hTr = sb("hTr", [P, 2, 16, P])
        ysb = sb("ysb", [P, 2, D])
        hfree = [hfree[0], hfree[1]]
        y_free = [m_b2]
        ht_free = [None, None]
        ys_free = [None, None]

        def routed(k):
            y = k % 2
            if k + 1 < NBLK:
                build_G(k + 1)
            hd = []
            for q in range(4):
                u = ("r", k, q, 0)
                un = number[u]
                b_ = q % 2
                PE.wait(hfree[b_], loaded[u], xg_ready[k])
                for jj in range(4):
                    for c in range(4):
                        f = lambda e, jj=jj, c=c, un=un, b_=b_: e.matmul(
                            bank[b_][:, P * jj:P * jj + P],
                            ring[:, un % NR, 512 * c + P * jj:512 * c + P * jj + P], xg[:, y, c, :],
                            start=(c == 0), stop=(c == 3))
                        m = PE.mark(f) if (jj == 3 and c == 3) else PE.do(f)
                ring_free[u] = m
                AC.wait(m, ht_free[y], (b1_land[k].sem, 16))
                for jj in range(4):
                    j = 4 * q + jj
                    f = lambda e, jj=jj, j=j, b_=b_: e.activation(hTr[:, y, j, :], bank[b_][:, P * jj:P * jj + P],
                                                                  ACT.Gelu, bias=b1r[:, k, j:j + 1])
                    mh = AC.mark(f) if jj == 3 else AC.do(f)
                hfree[b_] = mh
                hd.append(mh)
            xg_free[y] = m
            PE.wait(y_free[0])
            for q in range(4):
                u = ("r", k, q, 1)
                un = number[u]
                PE.wait(loaded[u], hd[q])
                for jj in range(4):
                    j = 4 * q + jj
                    f = lambda e, j=j, jj=jj, un=un: e.matmul(bank[2][:], hTr[:, y, j, :],
                                                              ring[:, un % NR, 512 * jj:512 * jj + 512],
                                                              start=(j == 0), stop=(j == 15))
                    m = PE.mark(f) if jj == 3 else PE.do(f)
                ring_free[u] = m
            ht_free[y] = m
            AC.wait(m, ys_free[y])
            y_free[0] = my = AC.mark(lambda e: e.copy(ysb[:, y, :], bank[2][:]))
            if k + 1 < NBLK:
                gather(k + 1)
                turn(k + 1)
            PE.wait(my, gwt_ready[k])
            for t in range(4):
                f = lambda e, t=t: e.matmul(bank[4 + t][:], GwT[:, y, t, :], ysb[:, y, :], start=False, stop=True,
                                            skip_group_check=True)
                m = PE.mark(f) if t == 3 else PE.do(f)
            gwt_free[y] = ys_free[y] = m

        for u in [u for u in units if u[0] == "r"]:
            n = number[u]
            loaded[u] = (ring_land[n % NR].sem, 16 * (n // NR + 1))
        for E in (AC, DVE):
            E.wait(y_done[3], xr_done[3])
        for k in range(NBLK):
            if k >= NE:
                for E in (PE, AC, DVE):
                    E.when(lambda k=k, E=E: regs["n", E.name] > k)
            routed(k)
            if k >= NE:
                for E in (PE, AC, DVE):
                    E.always()
        for k in range(NBLK):
            load_block(k)

        s_end, s_fin = sem("routed_done"), sem("sum_done")
        PE.do(lambda e: e.drain().then_inc(s_end, 1))
        DVE.do(lambda e: e.wait_ge(s_end, 1))
        for t in range(4):
            DVE.do(lambda e, t=t: e.tensor_tensor(xres[:, t, :], bank[4 + t][:], xres[:, t, :],
                                                  ALU.add).then_inc(s_fin, 1))
        c_out = landing("out")
        for t in range(4):
            SP.do(lambda e, t=t: e.wait_ge(s_fin, t + 1))
            mo = c_out.load(SP, out[t], xres[:, t, :])
        SP.wait(mo)

        block = st.enter_context(nc.Block())
        block.tensor(PE.emit)
        block.vector(DVE.emit)
        block.scalar(AC.emit)
        block.gpsimd(PL.emit)
        block.sync(SP.emit)


def kernel(**inputs):
    import numpy as np
    import concourse.bacc as bacc
    from concourse.bass_utils import run_bass_kernel_spmd as run

    a = {k: np.asarray(v) for k, v in inputs.items()}
    c = np.ascontiguousarray

    def rows(w):
        return c(w.reshape(4, P, -1).transpose(1, 0, 2))

    def spread(v):
        return c(np.broadcast_to(v.reshape(1, -1), (P, v.size)))

    ctxT = a["ctx_1024"].transpose(0, 2, 1).reshape(NB, 4, P, SKV).transpose(0, 2, 1, 3)
    arrays = {"x": c(a["x"].reshape(4, P, D).transpose(1, 0, 2))}
    for i, (k0, n) in enumerate(PARTS):
        arrays[f"ctx{i}"] = c(ctxT[:, :, :, k0:k0 + n]).reshape(NB, P, 4 * n)
    arrays["wq"] = rows(a["L0_xattn_Wq"].T)
    arrays["bq"] = c(a["L0_xattn_bq"].reshape(4, P).T)
    arrays["wk"] = rows(a["L0_xattn_Wk"].T)
    arrays["bk"] = c(a["L0_xattn_bk"].reshape(4, P).T)
    arrays["wv"] = rows(a["L0_xattn_Wv"].T)
    arrays["bv"] = c(np.broadcast_to(a["L0_xattn_bv"].reshape(4, P).T[:, :, None], (P, 4, 64)))
    arrays["wo"] = rows(a["L0_xattn_Wo"].T)
    arrays["bo"] = spread(a["L0_xattn_bo"])
    arrays["ak"] = rows(a["L0_attn_Wk"])
    arrays["av"] = rows(np.concatenate([a["L0_attn_Wv"]] * 2, axis=1))
    arrays["aq"] = rows(a["L0_attn_Wq"].transpose(1, 0, 2).reshape(D, D))
    arrays["ap_"] = rows(a["L0_attn_Wp"])
    arrays["abp"] = spread(a["L0_attn_bp"])
    arrays["rw"] = rows(a["L0_ffn_rW"])
    arrays["rb"] = spread(a["L0_ffn_rb"])
    w1 = np.concatenate([a["L0_ffn_W1"], a["L0_ffn_sW1"]])
    arrays["w1"] = c(w1.reshape(10, 4, P, 4, 512).transpose(0, 3, 2, 1, 4)).reshape(10, 4, P, 2048)
    b1 = np.concatenate([a["L0_ffn_b1"], a["L0_ffn_sb1"]])
    arrays["b1"] = c(b1.reshape(10, 16, P).transpose(0, 2, 1))
    w2 = np.concatenate([a["L0_ffn_W2"], a["L0_ffn_sW2"]])
    arrays["w2"] = c(w2.reshape(10, 4, 4, P, 512).transpose(0, 1, 3, 2, 4)).reshape(10, 4, P, 2048)
    arrays["b2"] = c(np.concatenate([a["L0_ffn_b2"], a["L0_ffn_sb2"]]))

    nc = bacc.Bacc("TRN2", target_bir_lowering=False, num_devices=1)
    args = {k: nc.dram_tensor("in_" + k, v.shape, mybir.dt.from_np(v.dtype), kind="ExternalInput").ap()
            for k, v in arrays.items()}
    o = nc.dram_tensor("out_0", (4, P, D), F32, kind="ExternalOutput").ap()
    build(nc, out=o, **args)
    r = run(nc, [{"in_" + k: v for k, v in arrays.items()}], core_ids=[0])
    return r.results[0]["out_0"].reshape(NB, NQ, D)
```

```python
from contextlib import ExitStack

import concourse.bass as bass
from concourse import mybir

F32 = mybir.dt.float32
F32R = mybir.dt.float32r
BF16 = mybir.dt.bfloat16
U32 = mybir.dt.uint32
I32 = mybir.dt.int32
ALU = mybir.AluOpType
ACT = mybir.ActivationFunctionType
AX = mybir.AxisListType

P = 128
D = 512
NB = 8
NQ = 64
SKV = 1601
PARTS = [(0, 256), (256, 256), (512, 256), (768, 256), (1024, 256), (1280, 321)]
NPT = len(PARTS)
WID = 322
EPS = 1e-5
XSCALE = float(32) ** -0.5
ASCALE = float(512) ** -0.5
NE = 8
HID = 2048
AT = {"S": 0.0, "T0": 0.369, "T1": 0.089, "LN": 0.484, "EX": 0.718, "F0": 1.21, "F1": 1.16, "DA": 2.041, "SH": 1.778, "SL": 2.021, "P": 2.584,
      "V": -2.33, "VH": -2.234, "VL": -1.934, "K": -0.916, "KH": -0.874, "KL": -0.482, "CH": -3.045, "CL": -1.884, "Q": -3.2, "O": 3.2, "R1": 0.25, "D": 3.3, "R": 3.6, "W": 5.05}


class Engine:

    def __init__(self, name, sem):
        self.name, self.sem, self.n, self.ops, self.seen = name, sem, 0, [], {}

    def wait(self, *marks):
        for m in marks:
            if m is None:
                continue
            sem, value = m
            if self.seen.get(id(sem), 0) >= value:
                continue
            self.seen[id(sem)] = value
            self.ops.append(lambda e, sem=sem, value=value: e.wait_ge(sem, value))

    def do(self, fn):
        self.ops.append(fn)

    def mark(self, fn):
        self.n += 1
        sem = self.sem
        self.ops.append(lambda e: fn(e).then_inc(sem, 1))
        return (sem, self.n)

    def when(self, cond):
        self.outer = self.ops
        self.ops = []
        self.outer.append((cond, self.ops))

    def always(self):
        self.ops = self.outer

    def emit(self, e, ops=None):
        for op in self.ops if ops is None else ops:
            if isinstance(op, tuple):
                with e.If(op[0]()):
                    self.emit(e, op[1])
            else:
                op(e)


class Landing:

    def __init__(self, sem):
        self.sem, self.n = sem, 0

    def load(self, q, dst, src):
        self.n += 16
        sem = self.sem
        q.do(lambda e: e.dma_start(dst, src).then_inc(sem, 16))
        return (sem, self.n)


def build(nc, x, ctx0, ctx1, ctx2, ctx3, ctx4, ctx5, wq, bq, wk, bk, wv, bv, wo, bo, ak, av, aq, ap_, abp, rw, rb,
          w1, b1, w2, b2, out):
    ctxs = [ctx0, ctx1, ctx2, ctx3, ctx4, ctx5]
    st = ExitStack()
    with st:
        def sb(name, shape, dt=F32):
            return st.enter_context(nc.sbuf_tensor(name, shape, dt))

        def sem(name):
            return st.enter_context(nc.semaphore(name))

        PE, DVE, AC, PL, SP = (Engine(n, sem("done_" + n)) for n in ("pe", "dve", "act", "pool", "sp"))

        def landing(name):
            return Landing(sem("load_" + name))

        bank = [st.enter_context(nc.psum_tensor(f"bank{i}", [P, 512], F32)) for i in range(8)]
        sc2 = None

        NR = 9
        VR = 6
        ident = sb("ident", [P, P])
        mask = sb("mask", [P, 64])
        iota8 = sb("iota8", [P, 8])
        iotai = sb("iotai", [P, 256], I32)
        epsb = sb("epsb", [P, 1])
        xres = sb("xres", [P, 4, D])
        xn = sb("xn", [P, 4, D])
        xT = sb("xT", [P, 4, D])
        stats = sb("stats", [P, 4, 6])
        mv = sb("mv", [P, 4, 2])
        sd = sb("sd", [P, 4])
        rstd = sb("rstd", [P, 4])
        bqt = sb("bqt", [P, 4])
        bqs = sb("bqs", [P, 4])
        bkt = sb("bkt", [P, 4])
        bvt = sb("bvt", [P, 4, 64])
        bot = sb("bot", [P, D])
        bpt = sb("bpt", [P, D])
        rbt = sb("rbt", [P, 8])
        rwt = sb("rwt", [P, 4, 8])
        b1s = sb("b1s", [P, 2, 16])
        iota128 = sb("iota128", [P, P])
        kio = sb("kio", [P, 15, 8])
        tri = sb("tri", [P, P], BF16)
        ones = sb("ones", [P, P], BF16)
        identb = sb("identb", [P, P], BF16)
        b2t = sb("b2t", [10, D])
        akt = sb("akt", [P, 4, 128])
        avt = sb("avt", [P, 4, 128])

        part1 = ExitStack()

        def sb1(name, shape, dt=F32):
            return part1.enter_context(nc.sbuf_tensor(name, shape, dt))

        wkh = sb1("wkh", [P, 4, D], F32R)
        wkl = sb1("wkl", [P, 4, D], F32R)
        wvh = sb1("wvh", [P, 4, D], F32R)
        wvl = sb1("wvl", [P, 4, D], F32R)
        cxh = sb1("cxh", [P, 2, 4, WID], F32R)
        cxl = sb1("cxl", [P, 2, 4, WID], F32R)
        ctxt = sb1("ctxt", [P, 2, 4 * WID])
        kh = sb1("kh", [P, 2, 4, WID], F32R)
        kl = sb1("kl", [P, 2, 4, WID], F32R)
        vh = sb1("vh", [P, VR, D], F32R)
        vl = sb1("vl", [P, VR, D], F32R)
        wqt = sb1("wqt", [P, 4, D])
        wot = wqt
        qc = sb1("qc", [P, 4, D])
        qbh = sb1("qbh", [P, 2, 4, 256], F32R)
        qbl = sb1("qbl", [P, 2, 4, 256], F32R)
        tt = sb1("tt", [P, 2, 1024])
        sh = sb1("sh", [P, 2, 1024], F32R)
        sl_ = sb1("sl", [P, 2, 1024], F32R)
        sel = sb1("sel", [P, 4, P])
        wkt = tt[:, :, :].rearrange("p a (c n) -> p (a c) n", c=2)
        wvt = qc
        dacc = xn[:, :, :].rearrange("p (a c) n -> p a (c n)", a=2)
        cU = xT[:, 0, :].rearrange("p (a g q) -> p a g q", a=2, g=4)
        rden = xT[:, 1, 0:256]
        cT = xT[:, 2, :].rearrange("p (g q) -> p g q", g=4)

        c_in, c_wq, c_wk, c_wv, c_sm = (landing(n) for n in ("in", "wq", "wk", "wv", "small"))
        m_wk = c_wk.load(SP, wkt, wk)
        c_ctx = [landing("ctx0"), landing("ctx1")]
        ctx_loaded = {}
        m_sm = None

        def load_ctx(i):
            b, s = divmod(i, NPT)
            n = PARTS[s][1]
            ctx_loaded[i] = c_ctx[i % 2].load(SP, ctxt[:, i % 2, 0:4 * n], ctxs[s][b])

        load_ctx(0)
        m_bk = landing("bk").load(SP, bkt[:], bk)
        m_x = c_in.load(SP, xres[:], x)
        m_wv = c_wv.load(SP, wvt[:], wv)
        m_wq = c_wq.load(SP, wqt[:], wq)
        load_ctx(1)
        for dst, src in ((bqt, bq), (bvt, bv), (bot, bo), (bpt, abp), (rbt, rb), (rwt, rw),
                         (b1s[:, 0, :], b1[8]), (b1s[:, 1, :], b1[9]), (b2t, b2), (akt, ak), (avt, av)):
            m_sm = c_sm.load(SP, dst[:] if hasattr(dst, "name") else dst, src)
        c_wo = landing("wo")

        z = PL.mark(lambda e: e.memset(ident[:], 0.0))
        PL.wait(z)
        z = m_id = PL.mark(lambda e: e.affine_select(out=ident[:], in_=ident[:], compare_op=ALU.not_equal, fill=1.0,
                                                 base=0, pattern=[[-1, P]], channel_multiplier=1))
        PL.wait(z)
        z = PL.mark(lambda e: e.memset(mask[:], 0.0))
        PL.wait(z)
        z = PL.mark(lambda e: e.affine_select(out=mask[0:64, :], in_=mask[0:64, :], compare_op=ALU.is_ge, fill=-1e30,
                                          base=0, pattern=[[-1, 64]], channel_multiplier=1))
        PL.wait(z)
        m_mask = PL.mark(lambda e: e.affine_select(out=mask[64:128, :], in_=mask[64:128, :], compare_op=ALU.is_ge,
                                                   fill=-1e30, base=0, pattern=[[-1, 64]], channel_multiplier=1))
        PL.wait(m_mask)
        z = PL.mark(lambda e: e.memset(ones[:], 1.0))
        PL.wait(z)
        z = PL.mark(lambda e: e.memset(tri[:], 1.0))
        PL.wait(z)
        z = PL.mark(lambda e: e.affine_select(out=tri[:], in_=tri[:], compare_op=ALU.is_ge, fill=0.0,
                                              base=-1, pattern=[[1, P]], channel_multiplier=-1))
        PL.wait(z)
        z = PL.mark(lambda e: e.iota(iotai[:, 0:P], pattern=[[1, P]], base=0, channel_multiplier=0))
        PL.wait(z)
        m_io = PL.mark(lambda e: e.iota(iotai[:, P:P + 120], pattern=[[1, 15], [0, 8]], base=0, channel_multiplier=0))
        PL.wait(m_io)
        z = PL.mark(lambda e: e.memset(qbh[:].bitcast(F32), 0.0))
        PL.wait(z)
        z = m_q0 = PL.mark(lambda e: e.memset(qbl[:].bitcast(F32), 0.0))
        PL.wait(z)
        z = PL.mark(lambda e: e.memset(sel[:], 0.0))
        for h in range(4):
            PL.wait(z)
            z = m_sel = PL.mark(lambda e, h=h: e.memset(sel[:, h, 32 * h:32 * h + 32], 1.0))
        for t_ in (cxh, cxl):
            for u in range(2):
                m_pad = DVE.mark(lambda e, t_=t_, u=u: e.memset(t_[:, u, :, 321:322].bitcast(F32), 0.0))
        m_eps = DVE.mark(lambda e: e.memset(epsb[:], EPS))
        DVE.wait(m_io)
        DVE.do(lambda e: e.tensor_copy(iota8[:], iotai[:, 0:8]))
        DVE.do(lambda e: e.tensor_copy(iota128[:], iotai[:, 0:P]))
        DVE.wait(m_id)
        m_idb = DVE.mark(lambda e: e.tensor_copy(identb[:], ident[:]))
        m_iota = DVE.mark(lambda e: e.tensor_copy(kio[:], iotai[:, P:P + 120].rearrange("p (k e) -> p k e", e=8)))

        AC.do(lambda e: e.preload_act_table_set("natural_log_exp_and_others"))

        def warm(n, bank_, *free):
            PE.wait(m_idb, *free)
            for _ in range(n):
                PE.do(lambda e: e.matmul(bank_[:, 0:P], identb[:], identb[:], start=True, stop=True,
                                         skip_group_check=True))

        def norm_stats(src, t, ready):
            DVE.wait(ready)
            m = DVE.mark(lambda e: e.bn_stats(stats[:, t, :], src[:, t, :]))
            DVE.wait(m)
            m = DVE.mark(lambda e: e.bn_aggr(mv[:, t, :], stats[:, t, :]))
            AC.wait(m, m_eps)
            m = AC.mark(lambda e: e.activation(sd[:, t:t + 1], mv[:, t, 1:2], ACT.Ln, bias=epsb[:, 0:1]))
            AC.wait(m)
            return AC.mark(lambda e: e.activation(rstd[:, t:t + 1], sd[:, t:t + 1], ACT.Exp, scale=-0.5))

        def norm_rows(src, t, m, *free):
            DVE.wait(m, *free)
            return DVE.mark(lambda e: e.tensor_scalar(xn[:, t, :], src[:, t, :], mv[:, t, 0:1],
                                                      rstd[:, t:t + 1], ALU.subtract, ALU.mult))

        def norm_turn(t, m, bank_, bank_free, *free):
            PE.wait(m, bank_free, m_id)
            for c in range(4):
                f = lambda e, c=c: e.transpose(bank_[:, c * P:(c + 1) * P], xn[:, t, c * P:(c + 1) * P], ident[:])
                m = PE.mark(f) if c == 3 else PE.do(f)
            E = (AC, DVE)[t % 2]
            E.wait(m, *free)
            dst, src = xT[:, :, t * P:(t + 1) * P], bank_[:].rearrange("p (c k) -> p c k", c=4)
            if E is AC:
                return E.mark(lambda e: e.copy(dst, src))
            return E.mark(lambda e: e.tensor_copy(dst, src))

        def layernorm(src, ready, banks, bank_free, between=None):
            rows = []
            for t in range(4):
                m = norm_stats(src, t, ready[t])
                if t:
                    rows.append(norm_rows(src, t - 1, m_))
                m_ = m
            rows.append(norm_rows(src, 3, m_))
            if between is not None:
                between()
            return [norm_turn(t, rows[t], banks[t], bank_free[t]) for t in range(4)], rows

        def split(hi, lo, src, ready, E_lo):
            AC.wait(*ready)
            mh = AC.mark(lambda e: e.copy(hi, src))
            E_lo.wait(*ready, mh)
            ml_ = E_lo.mark(lambda e: e.tensor_tensor(lo, src, hi.bitcast(F32), ALU.subtract))
            return mh, ml_

        for c in (slice(0, 2), slice(2, 4)):
            _, m_wks = split(wkh[:, c, :], wkl[:, c, :], wkt[:, c, :], [m_wk], DVE)
        chunks = [(b * NPT + s, k, min(P, PARTS[s][1] - k * P)) for b in range(NB) for s in range(NPT)
                  for k in range((PARTS[s][1] + P - 1) // P)]
        PER = len(chunks) // NB
        nparts = NPT * NB
        nchunks = len(chunks)
        first_of = {}
        for n_, (i_, k_, _) in enumerate(chunks):
            first_of.setdefault(i_, n_)

        def part_chunks(i):
            return (PARTS[i % NPT][1] + P - 1) // P

        M = {}

        def ctx_views(i):
            n, u = PARTS[i % NPT][1], i % 2
            return (ctxt[:, u, 0:4 * n].rearrange("p (c k) -> p c k", c=4), cxh[:, u, :, 0:n], cxl[:, u, :, 0:n])

        def ctx_hi(i):
            src, hi, lo = ctx_views(i)
            AC.wait(ctx_loaded[i], m_pad)
            if i >= 2:
                AC.wait(*[M["K", i - 2, g] for g in range(4)],
                        *[M["V", first_of[i - 2] + k] for k in range(part_chunks(i - 2))])
            M["CH", i] = AC.mark(lambda e: e.copy(hi, src))

        def ctx_lo(i, E=PL):
            src, hi, lo = ctx_views(i)
            E.wait(ctx_loaded[i], M["CH", i])
            M["CL", i] = E.mark(lambda e: e.tensor_tensor(lo, src, hi.bitcast(F32), ALU.subtract))
            if i + 2 < nparts:
                SP.wait(M["CL", i])
                load_ctx(i + 2)

        pj = [bank[0], bank[1]]
        pj_free = [None, None]
        pj_n = [0]
        pj_of = {}
        scb = [(bank[2], bank[3]), (bank[4], bank[5])]
        po = (bank[6], bank[7])
        dacc_m = [None]

        def take_pj():
            i = pj_n[0] % 2
            free, pj_free[i] = pj_free[i], "taken"
            assert free != "taken"
            pj_n[0] += 1
            return free, i

        def three(h, l):
            return ((h, 0), (h, 1), (l, 0))

        def keys(i, g):
            u, n = i % 2, PARTS[i % NPT][1]
            n += n % 2
            free, j = take_pj()
            pj_of[i, g, "k"] = j
            PE.wait(free, m_wks, M["CH", i], M["CL", i])
            for c in range(4):
                for x_, (w_, lo_) in enumerate(three(wkh, wkl)):
                    mv_ = (cxh, cxl)[lo_]
                    f = lambda e, c=c, w_=w_, mv_=mv_, x_=x_: e.matmul(
                        pj[j][:, 0:n], w_[:, c, g * P:(g + 1) * P], mv_[:, u, c, 0:n],
                        start=(c == 0 and x_ == 0), stop=(c == 3 and x_ == 2))
                    m = PE.mark(f) if (c == 3 and x_ == 2) else PE.do(f)
            M["K", i, g] = m

        def keys_hi(i, g):
            u, n, j = i % 2, PARTS[i % NPT][1], pj_of[i, g, "k"]
            AC.wait(M["K", i, g], m_bk)
            if i >= 2:
                AC.wait(M["S", first_of[i - 2] + part_chunks(i - 2) - 1, 1])
            M["KH", i, g] = AC.mark(lambda e: e.activation(kh[:, u, g, 0:n], pj[j][:, 0:n], ACT.Identity,
                                                           bias=bkt[:, g:g + 1]))

        def keys_lo(i, g):
            u, n, j = i % 2, PARTS[i % NPT][1], pj_of[i, g, "k"]
            DVE.wait(M["KH", i, g])
            M["KL", i, g] = pj_free[j] = DVE.mark(lambda e: e.scalar_tensor_tensor(
                kl[:, u, g, 0:n], pj[j][:, 0:n], bkt[:, g:g + 1], kh[:, u, g, 0:n].bitcast(F32),
                ALU.add, ALU.subtract))

        def values(n):
            i, k, kn = chunks[n]
            u = i % 2
            free, j = take_pj()
            pj_of[n, "v"] = j
            PE.wait(free, m_wvs, M["CH", i], M["CL", i])
            for c in range(4):
                for x_, (w_, lo_) in enumerate(three(cxh, cxl)):
                    mv_ = (wvh, wvl)[lo_]
                    f = lambda e, c=c, w_=w_, mv_=mv_, x_=x_: e.matmul(
                        pj[j][0:kn, :], w_[:, u, c, k * P:k * P + kn], mv_[:, c, :],
                        start=(c == 0 and x_ == 0), stop=(c == 3 and x_ == 2))
                    m = PE.mark(f) if (c == 3 and x_ == 2) else PE.do(f)
            M["V", n] = m

        def values_hi(n):
            kn, v, j = chunks[n][2], n % VR, pj_of[n, "v"]
            AC.wait(M["V", n])
            if n >= VR:
                AC.wait(M["P", n - VR])
            M["VH", n] = AC.mark(lambda e: e.copy(vh[0:kn, v, :], pj[j][0:kn, :]))

        def values_lo(n):
            kn, v, j = chunks[n][2], n % VR, pj_of[n, "v"]
            DVE.wait(M["VH", n])
            M["VL", n] = pj_free[j] = DVE.mark(lambda e: e.tensor_tensor(
                vl[0:kn, v, :], pj[j][0:kn, :], vh[0:kn, v, :].bitcast(F32), ALU.subtract))

        qb_ready = {}

        def batch_queries(b, h):
            y = b % 2
            if b >= 2:
                AC.wait(M["S", PER * (b - 1) - 1, 1])
            r = slice(32 * h, 32 * h + 32)
            AC.wait(*q_done, m_q0)
            mh = AC.mark(lambda e: e.copy(qbh[r, y, :, 64 * h:64 * h + 64], qc[r, :, 64 * b:64 * b + 64]))
            DVE.wait(mh, m_q0)
            m = DVE.mark(lambda e: e.tensor_tensor(
                qbl[r, y, :, 64 * h:64 * h + 64], qc[r, :, 64 * b:64 * b + 64],
                qbh[r, y, :, 64 * h:64 * h + 64].bitcast(F32), ALU.subtract))
            qb_ready[b] = (mh, m)

        def scores(n, hb):
            i, k, kn = chunks[n]
            u, w, b = i % 2, n % 2, i // NPT
            PE.wait(M["F", n - 2, hb] if n >= 2 else sc_free[w][hb], *qb_ready[b])
            for g in (2 * hb, 2 * hb + 1):
                PE.wait(M["KL", i, g])
                tgt = scb[w][hb][0:kn, 256 * (g % 2):256 * (g % 2) + 256]
                for x_, (k_, q_) in enumerate(((kh, qbh), (kh, qbl), (kl, qbh))):
                    f = lambda e, g=g, tgt=tgt, k_=k_, q_=q_, x_=x_: e.matmul(
                        tgt, k_[:, u, g, k * P:k * P + kn], q_[:, b % 2, g, :], start=(x_ == 0), stop=(x_ == 2))
                    m = PE.mark(f) if (g % 2 and x_ == 2) else PE.do(f)
            M["S", n, hb] = m

        def negatives(n, hb):
            kn, w, r = chunks[n][2], n % 2, slice(512 * hb, 512 * hb + 512)
            DVE.wait(M["S", n, hb])
            if n >= 2:
                DVE.wait(M["SL", n - 2], M["DA", n - 2])
            M["T", n, hb] = DVE.mark(lambda e: e.tensor_scalar(tt[0:kn, w, r], scb[w][hb][0:kn, :], -1.0, 0.0,
                                                               ALU.mult, ALU.max))

        def log1(n):
            kn, w = chunks[n][2], n % 2
            AC.wait(M["T", n, 0], M["T", n, 1])
            M["LN", n] = AC.mark(lambda e: e.activation(tt[0:kn, w, :], tt[0:kn, w, :], ACT.Ln, bias=1.0))

        def recip(n):
            kn, w = chunks[n][2], n % 2
            AC.wait(M["LN", n])
            M["EX", n] = AC.mark(lambda e: e.activation(tt[0:kn, w, :], tt[0:kn, w, :], ACT.Exp, scale=-1.0))

        def weights(n, hb):
            kn, w, r = chunks[n][2], n % 2, slice(512 * hb, 512 * hb + 512)
            DVE.wait(M["EX", n])
            M["F", n, hb] = DVE.mark(lambda e: e.scalar_tensor_tensor(
                tt[0:kn, w, r], scb[w][hb][0:kn, :], 0.0, tt[0:kn, w, r], ALU.max, ALU.add))

        def sums(n):
            kn, w, y = chunks[n][2], n % 2, (n // PER) % 2
            PL.wait(M["F", n, 0], M["F", n, 1], dacc_m[0])
            if n % PER == 0:
                PL.wait(dacc_free[y])
                dacc_m[0] = PL.mark(lambda e: e.tensor_copy(dacc[0:kn, y, :], tt[0:kn, w, :]))
            else:
                dacc_m[0] = PL.mark(lambda e: e.tensor_tensor(dacc[0:kn, y, :], dacc[0:kn, y, :], tt[0:kn, w, :],
                                                              ALU.add))
            M["DA", n] = dacc_m[0]

        def weights_hi(n):
            kn, w = chunks[n][2], n % 2
            DVE.wait(M["F", n, 0], M["F", n, 1])
            if n >= 2:
                DVE.wait(M["P", n - 2])
            M["SH", n] = DVE.mark(lambda e: e.tensor_copy(sh[0:kn, w, :], tt[0:kn, w, :]))

        def weights_lo(n):
            kn, w = chunks[n][2], n % 2
            DVE.wait(M["SH", n])
            M["SL", n] = DVE.mark(lambda e: e.tensor_tensor(
                sl_[0:kn, w, :], tt[0:kn, w, :], sh[0:kn, w, :].bitcast(F32), ALU.subtract))

        def weighted(n):
            kn, w = chunks[n][2], n % 2
            first, last = n % PER == 0, n % PER == PER - 1
            PE.wait(M["SL", n], M["VL", n])
            if first:
                PE.wait(*po_free)
            for g in range(4):
                for x_, (v_, s_) in enumerate(((vh, sh), (vh, sl_), (vl, sh))):
                    f = lambda e, g=g, v_=v_, s_=s_, x_=x_: e.matmul(
                        po[g // 2][:, 256 * (g % 2):256 * (g % 2) + 256],
                        v_[0:kn, n % VR, g * P:(g + 1) * P], s_[0:kn, w, 256 * g:256 * g + 256],
                        start=(first and g % 2 == 0 and x_ == 0), stop=(last and g % 2 == 1 and x_ == 2),
                        skip_group_check=True)
                    m = PE.mark(f) if (g == 3 and x_ == 2) else PE.do(f)
            M["P", n] = m

        x2_ready = [None] * 4

        def batch_out(b):
            y = b % 2
            mm = []
            for hb, E in ((0, DVE), (1, AC)):
                E.wait(M["P", PER * b + PER - 1], cU_free[y])
                src = po[hb][:, :].rearrange("p (g h q) -> p g h q", g=2, h=4)
                for h in range(4):
                    r = slice(32 * h, 32 * h + 32)
                    cp = (lambda e, o, i_: e.copy(o, i_)) if E is AC else (lambda e, o, i_: e.tensor_copy(o, i_))
                    f = lambda e, cp=cp, r=r, h=h, src=src, hb=hb: cp(e, cU[r, y, 2 * hb:2 * hb + 2, :],
                                                                      src[r, :, h, :])
                    po_free[hb] = E.mark(f)
                mm.append(po_free[hb])
            M["O", b] = mm

        def denominators(b):
            y = b % 2
            free, j = take_pj()
            PE.wait(free, M["DA", PER * b + PER - 1], m_sel)
            dv = dacc[:, y, :].rearrange("p (g h q) -> p g h q", g=4, h=4)
            for h in range(4):
                f = lambda e, h=h: e.matmul(pj[j][:, 0:256], sel[:, h, :], dv[:, :, h, :],
                                            start=(h == 0), stop=(h == 3))
                m = PE.mark(f) if h == 3 else PE.do(f)
            dacc_free[y] = m
            DVE.wait(m, M["C", b - 1] if b else ln1[1])
            M["D", b] = pj_free[j] = DVE.mark(lambda e: e.tensor_copy(rden, pj[j][:, 0:256]))

        def batch_ctx(b, g):
            y = b % 2
            rd = rden[:, 64 * g:64 * g + 64]
            DVE.wait(M["D", b], *M["O", b])
            m = DVE.mark(lambda e: e.reciprocal(rd, rd))
            DVE.wait(m, cT_free[0])
            m = DVE.mark(lambda e: e.tensor_tensor(cU[:, y, g, :], cU[:, y, g, :], rd, ALU.mult))
            DVE.wait(m, m_sm)
            M["C", b] = cU_free[y] = DVE.mark(lambda e: e.tensor_tensor(
                cT[:, g, 64 * y:64 * y + 64], cU[:, y, g, :], bvt[:, g, :], ALU.add))

        def batch_wo(b):
            t = b // 2
            free, j = take_pj()
            PE.wait(free, M["C", b], m_wo)
            for kk in range(4):
                f = lambda e, kk=kk: e.matmul(pj[j][:], cT[:, kk, :], wot[:, kk, :], start=(kk == 0), stop=(kk == 3))
                mo = PE.mark(f) if kk == 3 else PE.do(f)
            cT_free[0] = mo
            DVE.wait(mo, m_xr)
            x2_ready[t] = pj_free[j] = DVE.mark(lambda e: e.tensor_tensor(
                xres[:, t, :], pj[j][:], xres[:, t, :], ALU.add))

        ctx_hi(0)
        ctx_lo(0, DVE)
        m_wvs = None

        def first_keys():
            nonlocal m_wvs
            warm(30, bank[7])
            for g in range(4):
                keys(0, g)
                keys_hi(0, g)
                keys_lo(0, g)
                if g == 1:
                    _, m_wvs = split(wvh[:], wvl[:], wvt[:], [m_wv], DVE)
            for n in range(2):
                values(n)
                values_hi(n)
                values_lo(n)

        ln1, _ = layernorm(xres, [m_x] * 4, bank[2:6], [None] * 4, first_keys)
        ctx_hi(1)
        ctx_lo(1)
        DVE.wait(m_sm)
        m_bqs = DVE.mark(lambda e: e.tensor_scalar(bqs[:], bqt[:], XSCALE, None, ALU.mult))
        AC.wait(m_bqs, m_wvs)
        PE.wait(m_wq)
        q_done = []
        for g in range(4):
            bk_ = bank[(6, 7, 2, 3)[g]]
            if g > 1:
                PE.wait(ln1[g - 2])
            for c in range(4):
                PE.wait(*ln1)
                f = lambda e, g=g, c=c, bk_=bk_: e.matmul(bk_[:], wqt[:, c, g * P:(g + 1) * P], xT[:, c, :],
                                                          start=(c == 0), stop=(c == 3))
                m = PE.mark(f) if c == 3 else PE.do(f)
            AC.wait(m)
            q_done.append(AC.mark(lambda e, g=g, bk_=bk_: e.activation(qc[:, g, :], bk_[:], ACT.Identity,
                                                                      bias=bqs[:, g:g + 1], scale=XSCALE)))
        m_xT1 = m
        SP.wait(m)
        m_wo = c_wo.load(SP, wot[:], wo)
        for t in range(4):
            m_xr = DVE.mark(lambda e, t=t: e.tensor_tensor(xres[:, t, :], xres[:, t, :], bot[:], ALU.add))
        for h in range(4):
            batch_queries(0, h)
        po_free = [q_done[0], q_done[1]]
        sc_free = [[q_done[2], q_done[3]], [ln1[2], ln1[3]]]
        dacc_free = [m_xT1, m_xT1]
        cU_free = [m_xT1, m_xT1]
        cT_free = [m_xT1]

        plan = []
        stats2, rows2, ln2_done = [], [], []

        def early_stats(t):
            stats2.append(norm_stats(xres, t, x2_ready[t]))

        def warm_end():
            warm(60, bank[2], M["F", nchunks - 2, 0])

        def early_rows():
            for t in range(3):
                rows2.append(norm_rows(xres, t, stats2[t], dacc_free[0], dacc_free[1]))

        def put(at, fn, *args):
            plan.append((at, len(plan), fn, args))

        for n in range(nchunks):
            for hb in range(2):
                put(n + AT["S"], scores, n, hb)
                put(n + AT["T%d" % hb], negatives, n, hb)
                put(n + AT["F%d" % hb], weights, n, hb)
            put(n + AT["LN"], log1, n)
            put(n + AT["EX"], recip, n)
            put(n + AT["DA"], sums, n)
            put(n + AT["SH"], weights_hi, n)
            put(n + AT["SL"], weights_lo, n)
            put(n + AT["P"], weighted, n)
            if n >= 2:
                put(n + AT["V"], values, n)
                put(n + AT["VH"], values_hi, n)
                put(n + AT["VL"], values_lo, n)
        for i in range(1, nparts):
            n, w_ = first_of[i - 1], part_chunks(i - 1)
            for g in range(4):
                put(n + w_ * g / 4 + AT["K"], keys, i, g)
                put(n + w_ * g / 4 + AT["KH"], keys_hi, i, g)
                put(n + w_ * g / 4 + AT["KL"], keys_lo, i, g)
            if i >= 2:
                put(n + AT["CH"], ctx_hi, i)
                put(n + AT["CL"], ctx_lo, i)
        for b in range(NB):
            n = PER * b
            if b:
                for h in range(4):
                    put(n + AT["Q"] + h / 4, batch_queries, b, h)
            n += PER - 1
            put(n + AT["O"], batch_out, b)
            put(n + AT["D"], denominators, b)
            for g in range(4):
                put(n + AT["R"] + AT["R1"] * g, batch_ctx, b, g)
            if b % 2:
                if b == NB - 1:
                    put(n + AT["W"], early_rows)
                    put(n + AT["W"], warm_end)
                put(n + AT["W"], batch_wo, b)
                if b < NB - 1:
                    put(n + AT["W"] + 0.7, early_stats, b // 2)
        for _, _, fn, args in sorted(plan, key=lambda u: u[:2]):
            fn(*args)
        for t in range(3):
            ln2_done.append(norm_turn(t, rows2[t], bank[2 + t], M["F", nchunks - 2 + t // 2, t % 2], cT_free[0]))
        part1.close()
        NBLK = 15
        regs = {}
        p1_end = x2_ready[3]

        rows2.append(norm_rows(xres, 3, norm_stats(xres, 3, x2_ready[3])))
        ln2 = ln2_done + [norm_turn(3, rows2[3], bank[5], M["F", nchunks - 1, 1], cT_free[0])]
        ring = sb("ring", [P, NR, 2048])
        ring_land = [landing(f"ring{i}") for i in range(NR)]
        ring_free = {}
        units = [("s", e, q, kind) for e in (8, 9) for q in range(4) for kind in (0, 1)]
        units += [("r", k, q, kind) for k in range(NBLK) for kind in (0, 1) for q in range(4)]
        number = {u: n for n, u in enumerate(units)}
        loaded = {}

        aqt, apt = (ring[:, i, :].rearrange("p (c n) -> p c n", c=4) for i in range(2))
        ring_start = {}

        def slot(n):
            return (n + 2) % NR

        def load_unit(u):
            n = number[u]
            what, k, q, kind = u
            SP.wait(ring_free[units[n - NR]] if n >= NR else ring_start.get(n))
            src = (w1, w2)[kind]
            land = ring_land[slot(n)]
            if what == "s":
                loaded[u] = land.load(SP, ring[:, slot(n), :], src[k, q])
            else:
                land.n += 16
                SP.do(lambda e: e.dma_start(ring[:, slot(n), :], src[regs["e", k], q]).then_inc(land.sem, 16))
                loaded[u] = (land.sem, land.n)

        wsh = sb("wsh", [P, 3, 2048], F32R)
        wsl = sb("wsl", [P, 3, 2048], F32R)
        part2 = ExitStack()

        def sb2(name, shape, dt=F32):
            return part2.enter_context(nc.sbuf_tensor(name, shape, dt))

        K2 = sb2("K2", [P, 2, D])
        Q2 = sb2("Q2", [P, 2048])[:]
        V2 = sb2("V2", [P, 4, P])[:]
        sm = sb2("sm", [P, 2048])[:]
        pT = sb2("pT", [P, 2048])[:]
        oT = Q2
        SP.wait(*[M["K", nparts - 1, g] for g in range(4)], M["V", nchunks - 1])
        m_aq = ring_land[0].load(SP, aqt, aq)
        m_ap = ring_land[1].load(SP, apt, ap_)
        for u in units[:5]:
            load_unit(u)
        SP.wait(M["S", nchunks - 1, 1])
        for u in units[5:7]:
            load_unit(u)
        ws_ready, ws_free = {}, {}

        later = []

        def flush_loads():
            while later:
                n = later.pop(0)
                if units[n][0] == "s":
                    load_unit(units[n])

        def split_unit(n, E_lo=DVE):
            if n >= 16:
                return
            u = units[n]
            x_ = n % 3
            ready = [loaded[u], p1_end] + ([ws_free[n - 3]] if n >= 3 else [])
            mh, ml_ = split(wsh[:, x_, :], wsl[:, x_, :], ring[:, slot(n), :], ready, E_lo)
            ws_ready[n] = (mh, ml_)
            ring_free[u] = ml_
            later.append(n + NR)
            if n >= 3:
                flush_loads()

        mx = sb2("mx", [P, 32])
        rs = sb2("rs", [P, 32])
        PL.wait(p1_end)
        m_k0 = PL.mark(lambda e: e.memset(K2[:], 0.0))
        PE.wait(m_aq, m_sm)
        PE.wait(pj_free[0])
        for c in range(4):
            PE.wait(*ln2)
            f = lambda e, c=c: e.matmul(bank[0][:], akt[:, c, :], xT[:, c, :], start=(c == 0), stop=(c == 3))
            m = PE.mark(f) if c == 3 else PE.do(f)
        AC.wait(m)
        AC.wait(m_k0)
        AC.do(lambda e: e.copy(K2[0:64, 0, :], bank[0][0:64, :]))
        mk2 = AC.mark(lambda e: e.copy(K2[64:128, 1, :], bank[0][64:128, :]))
        Q2v = Q2.rearrange("p (b h t) -> p b h t", h=4, b=8)
        bfree = {2: ln2[0], 3: ln2[1], 4: ln2[2], 5: ln2[3], 6: po_free[0], 7: po_free[1]}
        mq2 = [None] * 4
        for h in range(4):
            bi = 2 + h
            PE.wait(bfree[bi])
            for c in range(4):
                f = lambda e, c=c, h=h, bi=bi: e.matmul(bank[bi][:], aqt[:, c, P * h:P * h + P], xT[:, c, :],
                                                        start=(c == 0), stop=(c == 3))
                m = PE.mark(f) if c == 3 else PE.do(f)
            ring_start[7] = m
            E = (AC, DVE)[h % 2]
            E.wait(m)
            dst = Q2v[:, :, h, :]
            src = bank[bi][:].rearrange("p (b t) -> p b t", b=8)
            if E is AC:
                mq2[h] = bfree[bi] = E.mark(lambda e, dst=dst, src=src: e.copy(dst, src))
            else:
                mq2[h] = bfree[bi] = E.mark(lambda e, dst=dst, src=src: e.tensor_copy(dst, src))
        load_unit(units[7])
        for n in range(3):
            split_unit(n, PL)
        PE.wait(mk2, *mq2)
        msc = []
        for bp in range(4):
            bi = 2 + bp
            PE.wait(bfree[bi])
            out_ = bank[bi][:].rearrange("p (r m b s) -> p r m b s", r=2, m=2, b=2)
            for b2_ in range(2):
                for mp in range(2):
                    b = 2 * bp + b2_
                    c0 = 256 * b + 128 * mp
                    f = lambda e, b=b, c0=c0, mp=mp, b2_=b2_, out_=out_: e.matmul(
                        out_[:, :, mp, b2_, :], Q2[:, c0:c0 + 128], K2[:, :, 64 * b:64 * b + 64],
                        start=True, stop=True)
                    m = PE.mark(f) if (b2_ and mp) else PE.do(f)
            msc.append(m)
        PE.wait(pj_free[1])
        for t in range(4):
            for c in range(4):
                f = lambda e, c=c, t=t: e.matmul(bank[1][:, 128 * t:128 * t + 128], xT[:, c, 128 * t:128 * t + 128],
                                                 avt[:, c, :], start=(c == 0), stop=(c == 3))
                m = PE.mark(f) if c == 3 else PE.do(f)
        AC.wait(m)
        mv2 = AC.mark(lambda e: e.copy(V2, bank[1][:].rearrange("p (t d) -> p t d", t=4)))
        mp_ = []
        DVE.wait(m_mask)
        for bp in range(4):
            sl = sm[:, 512 * bp:512 * bp + 512].rearrange("p (a s) -> p a s", s=64)
            ps = bank[2 + bp][:].rearrange("p (a s) -> p a s", s=64)
            a8 = slice(8 * bp, 8 * bp + 8)
            DVE.wait(msc[bp])
            m = bfree[2 + bp] = DVE.mark(lambda e, sl=sl, ps=ps: e.scalar_tensor_tensor(
                sl, ps, ASCALE, mask[:].unsqueeze(1).to_broadcast([P, 8, 64]), ALU.mult, ALU.add))
            DVE.wait(m)
            m = DVE.mark(lambda e, sl=sl, a8=a8: e.tensor_reduce(mx[:, a8], sl, AX.X, ALU.max))
            DVE.wait(m)
            m = DVE.mark(lambda e, a8=a8: e.tensor_scalar(mx[:, a8], mx[:, a8], -1.0, None, ALU.mult))
            AC.wait(m)
            for a in range(8):
                f = lambda e, sl=sl, a=a, bp=bp: e.activation(sl[:, a, :], sl[:, a, :], ACT.Exp,
                                                              bias=mx[:, 8 * bp + a:8 * bp + a + 1],
                                                              accum_out=rs[:, 8 * bp + a:8 * bp + a + 1])
                m = AC.mark(f) if a == 7 else AC.do(f)
            mp_.append(m)
        mn_ = []
        for bp in range(4):
            sl = sm[:, 512 * bp:512 * bp + 512].rearrange("p (a s) -> p a s", s=64)
            a8 = slice(8 * bp, 8 * bp + 8)
            DVE.wait(mp_[bp])
            m = DVE.mark(lambda e, a8=a8: e.reciprocal(rs[:, a8], rs[:, a8]))
            DVE.wait(m)
            mn_.append(DVE.mark(lambda e, sl=sl, a8=a8: e.tensor_tensor(
                sl, sl, rs[:, a8].unsqueeze(2).to_broadcast([P, 8, 64]), ALU.mult)))
        mpt = []
        for bp in range(4):
            bi = 2 + bp
            warm(60 if bp == 0 else 18, bank[7], po_free[1])
            PE.wait(bfree[bi], mn_[bp])
            for hp in range(4):
                f = lambda e, bp=bp, hp=hp, bi=bi: e.transpose(
                    bank[bi][:, 128 * hp:128 * hp + 128],
                    sm[:, 512 * bp + 128 * hp:512 * bp + 128 * hp + 128], ident[:])
                m = PE.mark(f) if hp == 3 else PE.do(f)
            AC.wait(m)
            mpt.append(AC.mark(lambda e, bp=bp, bi=bi: e.copy(pT[:, 512 * bp:512 * bp + 512], bank[bi][:])))
            bfree[bi] = mpt[-1]
        oTv = oT.rearrange("p (h k) -> p h k", h=4)
        PE.wait(mv2)
        bfree[0], bfree[1] = mk2, mv2
        mo_ = []
        for b in range(8):
            bi = (6, 7, 0, 1)[b % 4]
            r = slice(64 * (b % 2), 64 * (b % 2) + 64)
            PE.wait(bfree[bi], mpt[b // 2])
            m = PE.mark(lambda e, b=b, bi=bi, r=r: e.matmul(
                bank[bi][:], V2[r, b // 2, :], pT[r, 512 * (b // 2):512 * (b // 2) + 512], start=True, stop=True))
            E = (DVE, AC)[b % 2]
            E.wait(m)
            pv4 = bank[bi][:].rearrange("p (h x t) -> p h x t", h=4, x=2)
            for h2 in range(2):
                q = slice(64 * h2, 64 * h2 + 64)
                dst, src = oTv[q, :, 64 * b:64 * b + 64], pv4[q, :, h2, :]
                if E is AC:
                    m = E.mark(lambda e, dst=dst, src=src: e.copy(dst, src))
                else:
                    m = E.mark(lambda e, dst=dst, src=src: e.tensor_copy(dst, src))
            bfree[bi] = m
            mo_.append(m)
        x3_ready = []
        for t in range(4):
            m = DVE.mark(lambda e, t=t: e.tensor_tensor(xres[:, t, :], xres[:, t, :], bpt[:], ALU.add))
        DVE.wait(m)
        for t in range(4):
            bi = 2 + t
            PE.wait(bfree[bi], mo_[2 * t], mo_[2 * t + 1], m_ap)
            for hp in range(4):
                f = lambda e, t=t, hp=hp, bi=bi: e.matmul(bank[bi][:], oTv[:, hp, 128 * t:128 * t + 128],
                                                          apt[:, hp, :], start=(hp == 0), stop=(hp == 3))
                m = PE.mark(f) if hp == 3 else PE.do(f)
            DVE.wait(m)
            m = DVE.mark(lambda e, t=t, bi=bi: e.tensor_tensor(xres[:, t, :], bank[bi][:], xres[:, t, :], ALU.add))
            bfree[bi] = m
            x3_ready.append(m)

        p2_end = x3_ready[3]
        ring_start[8] = p2_end
        load_unit(units[8])
        flush_loads()
        ln3, ln3n = layernorm(xres, x3_ready, bank[0:4], [bfree[i] for i in range(4)])
        part2.close()
        wT = sb("wT", [10, 512])
        G = sb("G", [P, 2, 4, P], BF16)
        wb = sb("wb", [P, 2, 4, 3], BF16)
        wk_ = sb("wk_", [P, 3, 2, 4])
        wcol = sb("wcol", [P, 2])
        GA = xT[:, 0, :].rearrange("p (t k) -> p t k", t=4)
        GB = xT[:, 1, :].rearrange("p (t k) -> p t k", t=4)
        GT = sb("GT", [P, 2, 4, P], F32R)
        xb0 = (bot[:].bitcast(BF16), bpt[:].bitcast(BF16))
        xb12 = xn[:, :, :].bitcast(BF16)
        xb = [[xb0[t // 2][:, D * (t % 2):D * (t % 2) + D] for t in range(4)],
              [xb12[:, t, 0:D] for t in range(4)], [xb12[:, t, D:2 * D] for t in range(4)]]
        rest = avt[:, :, :].rearrange("p c n -> p (c n)")
        xg = xT[:, 2:4, :].rearrange("p a (t k) -> p a t k", t=4)
        b1r = sb("b1r", [P, NBLK, 16])
        gates = sb("gates", [P, 4, 8])
        top = sb("top", [P, 4, 8])
        tidx = sb("tidx", [P, 4, 8], U32)
        tif = sb("tif", [P, 4, 8])
        pr = sb("pr", [P, 4, 4])
        wts = sb("wts", [P, 4, 10])
        oh = sb("oh", [P, 2, 4, 8])
        ohw = sb("ohw", [P, 2, 4, 8])
        sel8 = sb("sel8", [P, 4, 8], BF16)
        cnt = sb("cnt", [P, 8])
        nbk = sb("nbk", [P, 2, 8])
        ends = sb("ends", [P, 3, 8])
        base = sb("base", [P, 8])
        gsl = sb("gsl", [P, 4, 8])
        gse = sb("gse", [P, 2, 4, 8])
        gs = sb("gs", [P, 2, 4])
        gsk = sb("gsk", [P, 2, 2, 4])
        kcmp = sb("kcmp", [P, 15, 8])
        kexp = sb("kexp", [P, 16])
        kint = sb("kint", [P, 16], I32)
        part3 = ExitStack()

        def sb3(name, shape, dt=F32):
            return part3.enter_context(nc.sbuf_tensor(name, shape, dt))

        xTh = sb3("xTh", [P, 4, D], F32R)
        xTl = sb3("xTl", [P, 4, D], F32R)
        hr = sb3("hr", [P, 2, D])
        hh = sb3("hh", [P, 4, D], F32R)
        hl = sb3("hl", [P, 4, D], F32R)

        x_split = []
        for c in range(4):
            AC.wait(*ln3)
            mh = AC.mark(lambda e, c=c: e.copy(xTh[:, c, :], xT[:, c, :]))
            DVE.wait(mh, *ln3)
            x_split += [mh, DVE.mark(lambda e, c=c: e.tensor_tensor(xTl[:, c, :], xT[:, c, :],
                                                                    xTh[:, c, :].bitcast(F32), ALU.subtract))]
        for t in range(4):
            PL.wait(*ln3, ln3n[t])
            z = PL.mark(lambda e, t=t: e.tensor_copy(xb[0][t], xn[:, t, :]))
            PL.wait(z)
            z = PL.mark(lambda e, t=t: e.tensor_tensor(rest, xn[:, t, :], xb[0][t], ALU.subtract))
            PL.wait(z)
            z = PL.mark(lambda e, t=t: e.tensor_copy(xb[1][t], rest))
            PL.wait(z)
            z = m_xb = PL.mark(lambda e, t=t: e.tensor_tensor(xb[2][t], rest, xb[1][t], ALU.subtract))
            PL.wait(z)
        PE.wait(ln3[2])
        for t in range(4):
            for c in range(4):
                PE.wait(*ln3)
                f = lambda e, t=t, c=c: e.matmul(bank[2][:, 8 * t:8 * t + 8], xT[:, c, 128 * t:128 * t + 128],
                                                 rwt[:, c, :], start=(c == 0), stop=(c == 3))
                m = PE.mark(f) if c == 3 else PE.do(f)
        m_gates = m

        def dve(fn, *waits):
            DVE.wait(chain[0], *waits)
            chain[0] = DVE.mark(fn)
            return chain[0]

        chain = [None]

        def route1():
            b_free2 = dve(lambda e: e.tensor_tensor(gates[:], bank[2][:, 0:32].rearrange("p (t e) -> p t e", t=4),
                                                    rbt[:].unsqueeze(1).to_broadcast([P, 4, 8]), ALU.add), m_gates)
            for t in range(4):
                dve(lambda e, t=t: e.max(top[:, t, :], gates[:, t, :]))
            for t in range(4):
                dve(lambda e, t=t: e.max_index(tidx[:, t, :], top[:, t, :], gates[:, t, :]))
            m = dve(lambda e: e.tensor_tensor(pr[:, :, 0], top[:, :, 1], top[:, :, 0], ALU.subtract))
            AC.wait(m)
            me = AC.mark(lambda e: e.activation(pr[:, :, 1], pr[:, :, 0], ACT.Exp))
            dve(lambda e: e.tensor_copy(tif[:], tidx[:]))
            for n_ in range(2):
                dve(lambda e, n_=n_: e.tensor_tensor(oh[:, n_, :, :], iota8[:].unsqueeze(1).to_broadcast([P, 4, 8]),
                                                     tif[:, :, n_:n_ + 1].to_broadcast([P, 4, 8]), ALU.is_equal))
            m_sel8 = dve(lambda e: e.tensor_tensor(sel8[:], oh[:, 0, :, :], oh[:, 1, :, :], ALU.add))
            dve(lambda e: e.tensor_scalar(pr[:, :, 2], pr[:, :, 1], 1.0, None, ALU.add), me)
            dve(lambda e: e.reciprocal(pr[:, :, 2], pr[:, :, 2]))
            dve(lambda e: e.tensor_tensor(pr[:, :, 3], pr[:, :, 2], pr[:, :, 1], ALU.mult))
            for n_ in range(2):
                dve(lambda e, n_=n_: e.tensor_tensor(ohw[:, n_, :, :], oh[:, n_, :, :],
                                                     pr[:, :, 2 + n_:3 + n_].to_broadcast([P, 4, 8]), ALU.mult))
            dve(lambda e: e.memset(wts[:], 0.5))
            m_w = dve(lambda e: e.tensor_tensor(wts[:, :, 0:8], ohw[:, 0, :, :], ohw[:, 1, :, :], ALU.add))
            return m_w, (m_sel8, b_free2)

        def places(m_sel8, b_free2):
            PE.wait(m_sel8, b_free2, m_io)
            for t in range(4):
                for t_ in range(t + 1):
                    f = lambda e, t=t, t_=t_: e.matmul(bank[2][:, 8 * t:8 * t + 8], (tri if t_ == t else ones)[:],
                                                       sel8[:, t_, :], start=(t_ == 0), stop=(t_ == t))
                    PE.do(f)
            for t_ in range(4):
                f = lambda e, t_=t_: e.matmul(bank[2][:, 32:40], ones[:], sel8[:, t_, :], start=(t_ == 0),
                                              stop=(t_ == 3))
                m_pos = PE.mark(f) if t_ == 3 else PE.do(f)
            return m_pos

        def block_count(E, m_int):
            E.wait(m_int)
            E.do(lambda e: regs.__setitem__(("n", E.name), e.value_load(kint[0:1, 15:16], min_val=0,
                                                                        max_val=NBLK)))

        def route2(m_pos, m_w):
            PE.wait(m_w, ln3[3])
            for t in range(4):
                f = lambda e, t=t: e.transpose(bank[3][0:10, 128 * t:128 * t + 128], wts[:, t, :], ident[:])
                m = PE.mark(f) if t == 3 else PE.do(f)
            AC.wait(m)
            m_wT = AC.mark(lambda e: e.copy(wT[:], bank[3][0:10, :]))
            dve(lambda e: e.tensor_copy(cnt[:], bank[2][:, 32:40]), m_pos)
            dve(lambda e: e.tensor_scalar(nbk[:, 0, :], cnt[:], 0.0, None, ALU.is_gt))
            for n_ in range(3):
                dve(lambda e, n_=n_: e.scalar_tensor_tensor(nbk[:, (n_ + 1) % 2, :], cnt[:], 128.0 * (n_ + 1),
                                                            nbk[:, n_ % 2, :], ALU.is_gt, ALU.add))
            src = nbk[:, 1, :]
            for n_, d in enumerate((1, 2, 4)):
                dve(lambda e, n_=n_, d=d, src=src: e.tensor_copy(ends[:, n_, 0:d], src[:, 0:d]))
                dve(lambda e, n_=n_, d=d, src=src: e.tensor_tensor(ends[:, n_, d:8], src[:, d:8], src[:, 0:8 - d],
                                                                   ALU.add))
                src = ends[:, n_, :]
            end = ends[:, 2, :]
            dve(lambda e: e.tensor_tensor(kcmp[:], kio[:], end.unsqueeze(1).to_broadcast([P, 15, 8]), ALU.is_ge))
            dve(lambda e: e.tensor_reduce(kexp[:, 0:15], kcmp[:], AX.X, ALU.add))
            dve(lambda e: e.tensor_scalar(kexp[:, 0:15], kexp[:, 0:15], 7.0, None, ALU.min))
            dve(lambda e: e.tensor_copy(kexp[:, 15:16], end[:, 7:8]))
            m_int = dve(lambda e: e.tensor_copy(kint[:], kexp[:]))
            dve(lambda e: e.tensor_tensor(base[:], end, nbk[:, 1, :], ALU.subtract))
            m_b2 = dve(lambda e: e.scalar_tensor_tensor(gsl[:], base[:].unsqueeze(1).to_broadcast([P, 4, 8]), 128.0,
                                                        bank[2][:, 0:32].rearrange("p (t e) -> p t e", t=4),
                                                        ALU.mult, ALU.add))
            dve(lambda e: e.tensor_tensor(gse[:], oh[:], gsl[:].unsqueeze(1).to_broadcast([P, 2, 4, 8]), ALU.mult))
            dve(lambda e: e.tensor_reduce(gs[:], gse[:], AX.X, ALU.add))
            block_count(SP, m_int)
            return m_wT, m_b2, m_int

        bank3_free = [None]
        G_free = [None, None]
        xg_ready, gwt_ready = {}, {}
        xg_free, gwt_free = [None, None], [None, None]
        g_marks = {}

        def build_G(k):
            y = k % 2
            dve(lambda e: e.tensor_scalar(gsk[:, y, :, :], gs[:], -128.0 * k, None, ALU.add))
            io = iota128[:].unsqueeze(1).to_broadcast([P, 4, P])
            for n_, X in ((0, GA), (1, GB)):
                dve(lambda e, n_=n_, X=X: e.tensor_tensor(X, io, gsk[:, y, n_, :].unsqueeze(2).to_broadcast(
                    [P, 4, P]), ALU.is_equal), m_gates)
            dve(lambda e: e.tensor_tensor(G[:, y, :, :], GA, GB, ALU.add), G_free[y])
            a_, b_, c_ = wk_[:, 0, :, :], wk_[:, 1, :, :], wk_[:, 2, 0, :]
            dve(lambda e: e.tensor_scalar(a_, gsk[:, y, :, :], 0.0, None, ALU.is_ge))
            dve(lambda e: e.scalar_tensor_tensor(b_, gsk[:, y, :, :], 128.0, a_, ALU.is_lt, ALU.mult))
            dve(lambda e: e.tensor_tensor(a_, b_, pr[:, :, 2:4].rearrange("p t n -> p n t"), ALU.mult))
            dve(lambda e: e.tensor_tensor(c_, wk_[:, 0, 0, :], wk_[:, 0, 1, :], ALU.add))
            dve(lambda e: e.tensor_copy(wb[:, y, :, 0], c_))
            dve(lambda e: e.tensor_tensor(c_, c_, wb[:, y, :, 0], ALU.subtract))
            dve(lambda e: e.tensor_copy(wb[:, y, :, 1], c_))
            g_marks[k] = dve(lambda e: e.tensor_tensor(wb[:, y, :, 2], c_, wb[:, y, :, 1], ALU.subtract))

        def gather(k):
            y = k % 2
            PE.wait(g_marks[k], m_xb, bank3_free[0])
            for c in range(4):
                for t in range(4):
                    for s_ in range(3):
                        f = lambda e, c=c, t=t, s_=s_: e.matmul(
                            bank[3][:, P * c:P * c + P], xb[s_][t][:, P * c:P * c + P], G[:, y, t, :],
                            start=(t == 0 and s_ == 0), stop=(t == 3 and s_ == 2))
                        m = PE.mark(f) if (c == 3 and t == 3 and s_ == 2) else PE.do(f)
            DVE.wait(m, xg_free[y])
            xg_ready[k] = bank3_free[0] = DVE.mark(lambda e: e.tensor_copy(
                xg[:, y, :, :], bank[3][:].rearrange("p (c k) -> p c k", c=4)))

        def turn(k, ba, fa, bb, fb):
            y = k % 2
            PE.wait(g_marks[k], fa[0][fa[1]])
            for t in range(4):
                f = lambda e, t=t: e.matmul(ba[:, P * t:P * t + P], G[:, y, t, :], identb[:], start=True, stop=True)
                m = PE.mark(f) if t == 3 else PE.do(f)
            AC.wait(m, gwt_free[y])
            gwt_ready[k] = fa[0][fa[1]] = AC.mark(lambda e: e.copy(
                GT[:, y, :, :], ba[:].rearrange("p (c k) -> p c k", c=4)))
            PE.wait(fb[0][fb[1]])
            for t in range(4):
                f = lambda e, t=t: e.matmul(bb[:, 0:3], G[:, y, t, :], wb[:, y, t, :], start=(t == 0), stop=(t == 3))
                m = PE.mark(f) if t == 3 else PE.do(f)
            G_free[y] = m
            DVE.wait(m, gwt_free[y])
            w_ready[k] = fb[0][fb[1]] = DVE.mark(lambda e: e.tensor_reduce(wcol[:, y:y + 1], bb[:, 0:3], AX.X,
                                                                           ALU.add))

        w_ready = {}

        def load_block(k):
            if k >= NE:
                SP.when(lambda k=k: regs["n", "sp"] > k)
            SP.do(lambda e: regs.__setitem__(("e", k), e.value_load(kint[0:1, k:k + 1], min_val=0, max_val=7)))
            m = b1_land[k]
            SP.do(lambda e: e.dma_start(b1r[:, k, :], b1[regs["e", k]]).then_inc(m.sem, 16))
            for kind in (0, 1):
                for q in range(4):
                    load_unit(("r", k, q, kind))
            if k >= NE:
                SP.always()

        b1_land = [landing(f"b1_{k}") for k in range(NBLK)]

        hfree = [ln3[0], ln3[1]]
        h_done, hb_free = {}, {}
        order = [(e_, j) for e_ in range(2) for j in range(16)]

        def hid(n):
            e_, j = order[n]
            q, jj = divmod(j, 4)
            un = number["s", 8 + e_, q, 0]
            b_, r_ = n % 2, n % 4
            PE.wait(hfree[b_], *ws_ready[un], *x_split)
            k_ = 0
            for c in range(4):
                for w_, x_ in ((wsh, xTh), (wsh, xTl), (wsl, xTh)):
                    f = lambda e, c=c, w_=w_, x_=x_, k_=k_: e.matmul(
                        bank[b_][:], w_[:, un % 3, 512 * c + 128 * jj:512 * c + 128 * jj + 128], x_[:, c, :],
                        start=(k_ == 0), stop=(k_ == 11))
                    m = PE.mark(f) if k_ == 11 else PE.do(f)
                    k_ += 1
            if jj == 3:
                ws_free[un] = m
            AC.wait(m, h_done.get(n - 2))
            hfree[b_] = mg = AC.mark(lambda e: e.activation(hr[:, n % 2, :], bank[b_][:], ACT.Gelu,
                                                            bias=b1s[:, e_, j:j + 1]))
            DVE.wait(mg, hb_free.get(n - 4))
            mh = DVE.mark(lambda e: e.tensor_copy(hh[:, r_, :], hr[:, n % 2, :]))
            DVE.wait(mh)
            h_done[n] = DVE.mark(lambda e: e.tensor_tensor(hl[:, r_, :], hr[:, n % 2, :], hh[:, r_, :].bitcast(F32),
                                                           ALU.subtract))
            return un if jj == 3 else None

        def down(n):
            e_, j = order[n]
            q, jj = divmod(j, 4)
            un = number["s", 8 + e_, q, 1]
            r_ = n % 4
            PE.wait(*ws_ready[un], h_done[n])
            if n == 0:
                PE.wait(*[bfree[i] for i in range(4, 8)])
            for t in range(4):
                for k_, (h_, w_) in enumerate(((hh, wsh), (hh, wsl), (hl, wsh))):
                    f = lambda e, t=t, k_=k_, h_=h_, w_=w_: e.matmul(
                        bank[4 + t][:], h_[:, r_, P * t:P * t + P], w_[:, un % 3, 512 * jj:512 * jj + 512],
                        start=(n == 0 and k_ == 0), stop=(n == 31 and k_ == 2))
                    m = PE.mark(f) if k_ == 2 else PE.do(f)
                if n == 31:
                    y_done.append(m)
            hb_free[n] = m
            if jj == 3:
                ws_free[un] = m
            return un if jj == 3 else None

        y_done = []
        m_w, m_sel = route1()
        nsplit = 3
        LAG = 3
        for n in range(32 + LAG):
            d1 = hid(n) if n < 32 else None
            if n == 1:
                m_pos = places(*m_sel)
            if n == 3:
                m_wT, m_b2, m_int = route2(m_pos, m_w)
            if n == 4:
                build_G(0)
            if n == 6:
                bank3_free[0] = m_wT
                gather(0)
                turn(0, bank[3], (bank3_free, 0), bank[3], (bank3_free, 0))
            if d1 is not None and nsplit - 3 in ws_free:
                split_unit(nsplit)
                nsplit += 1
            d2 = down(n - LAG) if n >= LAG else None
            while nsplit < 16 and nsplit - 3 in ws_free:
                split_unit(nsplit)
                nsplit += 1
        xr_done = []
        for t in range(4):
            DVE.wait(y_done[t])
            xr_done.append(DVE.mark(lambda e, t=t: e.scalar_tensor_tensor(xres[:, t, :], bank[4 + t][:], 0.5,
                                                                          xres[:, t, :], ALU.mult, ALU.add)))
            PE.wait(xr_done[t], m_wT)
            PE.do(lambda e, t=t: e.matmul(bank[4 + t][:], wT[:, P * t:P * t + P], b2t[:], start=True, stop=True,
                                          skip_group_check=True))
        part3.close()
        hg = sb("hg", [P, 2, D])
        hTh = sb("hTh", [P, 16, P], F32R)
        hTl = sb("hTl", [P, 16, P], F32R)
        yh = sb("yh", [P, 2, D], F32R)
        yl = sb("yl", [P, 2, D], F32R)
        y_free = [m_b2]
        ht_free = [None]
        ys_free = [None, None]
        hg_free = [None, None]

        def routed(k):
            y = k % 2
            hd = []

            def split_w2(q):
                u = ("r", k, q, 1)
                r_ = 16 + 4 * k + q
                ws_ready[r_] = split(wsh[:, r_ % 3, :], wsl[:, r_ % 3, :], ring[:, slot(number[u]), :],
                                     [loaded[u], ws_free[r_ - 3]], DVE)
                ring_free[u] = ws_ready[r_][1]

            for q in range(4):
                u = ("r", k, q, 0)
                un = number[u]
                b_ = q % 2
                PE.wait(hfree[b_], loaded[u], xg_ready[k])
                for jj in range(4):
                    for c in range(4):
                        f = lambda e, jj=jj, c=c, un=un, b_=b_: e.matmul(
                            bank[b_][:, P * jj:P * jj + P],
                            ring[:, slot(un), 512 * c + P * jj:512 * c + P * jj + P], xg[:, y, c, :],
                            start=(c == 0), stop=(c == 3))
                        m = PE.mark(f) if (jj == 3 and c == 3) else PE.do(f)
                ring_free[u] = m
                if q < 3:
                    split_w2(q)
                AC.wait(m, hg_free[b_], (b1_land[k].sem, 16))
                for jj in range(4):
                    j = 4 * q + jj
                    f = lambda e, jj=jj, j=j, b_=b_: e.activation(hg[:, b_, P * jj:P * jj + P],
                                                                  bank[b_][:, P * jj:P * jj + P],
                                                                  ACT.Gelu, bias=b1r[:, k, j:j + 1])
                    mh = AC.mark(f) if jj == 3 else AC.do(f)
                hfree[b_] = mh
                DVE.wait(mh, ht_free[0])
                hv = hg[:, b_, :].rearrange("p (j n) -> p j n", j=4)
                m1 = DVE.mark(lambda e, q=q, hv=hv: e.tensor_copy(hTh[:, 4 * q:4 * q + 4, :], hv))
                DVE.wait(m1)
                hg_free[b_] = m1 = DVE.mark(lambda e, q=q, hv=hv: e.tensor_tensor(
                    hTl[:, 4 * q:4 * q + 4, :], hv, hTh[:, 4 * q:4 * q + 4, :].bitcast(F32), ALU.subtract))
                hd.append(m1)
                if q == 1 and k + 1 < NBLK:
                    build_G(k + 1)
            xg_free[y] = m
            PE.wait(y_free[0])
            for q in range(4):
                r_ = 16 + 4 * k + q
                if r_ not in ws_ready:
                    split_w2(q)
                PE.wait(hd[q], *ws_ready[r_])
                for jj in range(4):
                    j = 4 * q + jj
                    for x_, (h_, w_) in enumerate(((hTh, wsh), (hTh, wsl), (hTl, wsh))):
                        f = lambda e, j=j, jj=jj, r_=r_, h_=h_, w_=w_, x_=x_: e.matmul(
                            bank[2][:], h_[:, j, :], w_[:, r_ % 3, 512 * jj:512 * jj + 512],
                            start=(j == 0 and x_ == 0), stop=(j == 15 and x_ == 2))
                        m = PE.mark(f) if (jj == 3 and x_ == 2) else PE.do(f)
                ws_free[r_] = m
            ht_free[0] = m
            AC.wait(m, ys_free[y], w_ready[k])
            mh = AC.mark(lambda e: e.activation(yh[:, y, :], bank[2][:], ACT.Identity, scale=wcol[:, y:y + 1]))
            DVE.wait(mh, w_ready[k])
            y_free[0] = my = DVE.mark(lambda e: e.scalar_tensor_tensor(
                yl[:, y, :], bank[2][:], wcol[:, y:y + 1], yh[:, y, :].bitcast(F32), ALU.mult, ALU.subtract))
            if k + 1 < NBLK:
                gather(k + 1)
                turn(k + 1, bank[1], (hfree, 1), bank[0], (hfree, 0))
            PE.wait(my, gwt_ready[k])
            for t in range(4):
                for x_, y_ in enumerate((yh, yl)):
                    f = lambda e, t=t, y_=y_: e.matmul(bank[4 + t][:], GT[:, y, t, :], y_[:, y, :], start=False,
                                                       stop=True, skip_group_check=True)
                    m = PE.mark(f) if (t == 3 and x_) else PE.do(f)
            gwt_free[y] = ys_free[y] = m

        for u in [u for u in units if u[0] == "r"]:
            n = number[u]
            loaded[u] = (ring_land[slot(n)].sem, 16 * ((n + 2) // NR + 1))
        for E in (AC, DVE):
            E.wait(y_done[3], xr_done[3])
        for E in (PE, AC, DVE):
            block_count(E, m_int)
        for k in range(NBLK):
            if k >= NE:
                for E in (PE, AC, DVE):
                    E.when(lambda k=k, E=E: regs["n", E.name] > k)
            routed(k)
            if k >= NE:
                for E in (PE, AC, DVE):
                    E.always()
        for k in range(NBLK):
            load_block(k)

        s_end, s_fin = sem("routed_done"), sem("sum_done")
        PE.do(lambda e: e.drain().then_inc(s_end, 1))
        DVE.do(lambda e: e.wait_ge(s_end, 1))
        for t in range(4):
            DVE.do(lambda e, t=t: e.tensor_tensor(xres[:, t, :], bank[4 + t][:], xres[:, t, :],
                                                  ALU.add).then_inc(s_fin, 1))
        c_out = landing("out")
        for t in range(4):
            SP.do(lambda e, t=t: e.wait_ge(s_fin, t + 1))
            mo = c_out.load(SP, out[t], xres[:, t, :])
        SP.wait(mo)

        block = st.enter_context(nc.Block())
        block.tensor(PE.emit)
        block.vector(DVE.emit)
        block.scalar(AC.emit)
        block.gpsimd(PL.emit)
        block.sync(SP.emit)


def kernel(**inputs):
    import numpy as np
    import concourse.bacc as bacc
    from concourse.bass_utils import run_bass_kernel_spmd as run

    a = {k: np.asarray(v) for k, v in inputs.items()}
    c = np.ascontiguousarray

    def rows(w):
        return c(w.reshape(4, P, -1).transpose(1, 0, 2))

    def spread(v):
        return c(np.broadcast_to(v.reshape(1, -1), (P, v.size)))

    ctxT = a["ctx_1024"].transpose(0, 2, 1).reshape(NB, 4, P, SKV).transpose(0, 2, 1, 3)
    arrays = {"x": c(a["x"].reshape(4, P, D).transpose(1, 0, 2))}
    for i, (k0, n) in enumerate(PARTS):
        arrays[f"ctx{i}"] = c(ctxT[:, :, :, k0:k0 + n]).reshape(NB, P, 4 * n)
    arrays["wq"] = rows(a["L0_xattn_Wq"].T)
    arrays["bq"] = c(a["L0_xattn_bq"].reshape(4, P).T)
    arrays["wk"] = rows(a["L0_xattn_Wk"].T)
    arrays["bk"] = c(a["L0_xattn_bk"].reshape(4, P).T)
    arrays["wv"] = rows(a["L0_xattn_Wv"].T)
    arrays["bv"] = c(np.broadcast_to(a["L0_xattn_bv"].reshape(4, P).T[:, :, None], (P, 4, 64)))
    arrays["wo"] = rows(a["L0_xattn_Wo"].T)
    arrays["bo"] = spread(a["L0_xattn_bo"])
    arrays["ak"] = rows(np.concatenate([a["L0_attn_Wk"]] * 2, axis=1))
    arrays["av"] = rows(np.concatenate([a["L0_attn_Wv"]] * 2, axis=1))
    arrays["aq"] = rows(a["L0_attn_Wq"].transpose(1, 0, 2).reshape(D, D))
    arrays["ap_"] = rows(a["L0_attn_Wp"].reshape(4, 2, 64, D).transpose(1, 0, 2, 3).reshape(D, D))
    arrays["abp"] = spread(a["L0_attn_bp"])
    arrays["rw"] = rows(a["L0_ffn_rW"])
    arrays["rb"] = spread(a["L0_ffn_rb"])
    w1 = np.concatenate([a["L0_ffn_W1"], a["L0_ffn_sW1"]])
    arrays["w1"] = c(w1.reshape(10, 4, P, 4, 512).transpose(0, 3, 2, 1, 4)).reshape(10, 4, P, 2048)
    b1 = np.concatenate([a["L0_ffn_b1"], a["L0_ffn_sb1"]])
    arrays["b1"] = c(b1.reshape(10, 16, P).transpose(0, 2, 1))
    w2 = np.concatenate([a["L0_ffn_W2"], a["L0_ffn_sW2"]])
    arrays["w2"] = c(w2.reshape(10, 4, 4, P, 512).transpose(0, 1, 3, 2, 4)).reshape(10, 4, P, 2048)
    arrays["b2"] = c(np.concatenate([a["L0_ffn_b2"], a["L0_ffn_sb2"]]))

    nc = bacc.Bacc("TRN2", target_bir_lowering=False, num_devices=1)
    args = {k: nc.dram_tensor("in_" + k, v.shape, mybir.dt.from_np(v.dtype), kind="ExternalInput").ap()
            for k, v in arrays.items()}
    o = nc.dram_tensor("out_0", (4, P, D), F32, kind="ExternalOutput").ap()
    build(nc, out=o, **args)
    r = run(nc, [{"in_" + k: v for k, v in arrays.items()}], core_ids=[0])
    return r.results[0]["out_0"].reshape(NB, NQ, D)
```
